# Optimizing a Trainium2 kernel written in Bass

```python
import numpy as np
import jax
import jax.numpy as jnp

def _softmax(x, axis=-1):
    return jax.nn.softmax(x, axis=axis)

def _gelu(x):
    return jax.nn.gelu(x, approximate=True)

def _silu(x):
    return jax.nn.silu(x)

def _sigmoid(x):
    return jax.nn.sigmoid(x)

def _layernorm(x, axis=-1, eps=1e-05):
    m = jnp.mean(x, axis=axis, keepdims=True)
    v = jnp.var(x, axis=axis, keepdims=True)
    return (x - m) / jnp.sqrt(v + eps)

def _scatter_add(tgt, idx, src, axis=0):
    return tgt.at[idx].add(src)

def _segment_sum(src, seg, n):
    return jax.ops.segment_sum(src, seg, n)
kernel_name = 'mk_decoder_postln_d1_seqx_r8_621461'

def setup_inputs(seed: int=0):
    np.random.seed(seed)
    _w = jnp.asarray

    def _rec_inputs():
        import jax
        import jax.numpy as jnp
        _rk = jax.random.key(seed)
        x = -0.0002928 + 1 * jax.random.normal(jax.random.fold_in(_rk, 1), (128, 64, 128), jnp.float32)
        _lenS = 64 - jax.random.randint(jax.random.fold_in(_rk, 7), (128,), 0, max(1, 64 // 4) + 1, jnp.int32)
        _lenS2 = 64 - jax.random.randint(jax.random.fold_in(_rk, 8), (128,), 0, max(1, 64 // 4) + 1, jnp.int32)
        _ctx_1024P = jax.random.normal(jax.random.fold_in(_rk, 11), (128, 16, 128), jnp.float32)
        _ctx_1024c = jax.random.dirichlet(jax.random.fold_in(_rk, 511), 0.3 * jnp.ones((16,), jnp.float32), (128, 64))
        _ctx_1024t = jnp.einsum('bsk,bkd->bsd', _ctx_1024c, _ctx_1024P)
        _ctx_1024t = _ctx_1024t * jax.lax.rsqrt(jnp.mean(jnp.square(_ctx_1024t)) + 1e-12) * 0.953939
        ctx_1024 = -1.39393e-06 + 0.999914 * (_ctx_1024t + 0.3 * jax.random.normal(jax.random.fold_in(_rk, 611), (128, 64, 128), jnp.float32))
        return (x, ctx_1024)
    x, ctx_1024 = _rec_inputs()

    def _L0_attn_setup():
        import jax, jax.numpy as jnp
        import numpy as np
        N_HEADS = 16
        key = jax.random.key(seed)
        k_x, k_q, k_k, k_v, k_o = jax.random.split(key, 5)
        N, S, D = (8, 512, 128)
        scale = 0.02
        return {'x': jax.random.normal(k_x, (N, S, D), dtype=jnp.float32), 'Wq': jax.random.normal(k_q, (D, D), dtype=jnp.float32) * scale, 'Wk': jax.random.normal(k_k, (D, D), dtype=jnp.float32) * scale, 'Wv': jax.random.normal(k_v, (D, D), dtype=jnp.float32) * scale, 'Wo': jax.random.normal(k_o, (D, D), dtype=jnp.float32) * scale, 'bo': jnp.zeros((D,), dtype=jnp.float32)}
    _L0_attn_all = _L0_attn_setup()
    _L0_attn_in = {k: v for k, v in _L0_attn_all.items() if k in ('Wq', 'Wk', 'Wv', 'Wo', 'bo')}
    del _L0_attn_all

    def _L0_xattn_setup():
        import jax, jax.numpy as jnp
        import numpy as np
        import math
        HIDDEN = 128
        HEADS = 16
        HEAD = HIDDEN // HEADS
        SCALE_BASE = 512.0

        def _gammas(heads):
            return 1.0 - jnp.exp(jnp.linspace(math.log(1.0 / 32.0), math.log(1.0 / 512.0), heads))

        def _xpos(x, downscale):
            S, d = (x.shape[2], x.shape[3])
            half = d // 2
            base_scale = (jnp.arange(0, d, 2, dtype=jnp.float32) + 0.4 * d) / (1.4 * d)
            pos = jnp.arange(S, dtype=jnp.float32)
            scale = base_scale[None, :] ** (pos / SCALE_BASE)[:, None]
            if downscale:
                scale = 1.0 / scale
            inv_freq = 1.0 / 10000.0 ** (jnp.arange(half, dtype=jnp.float32) / half)
            sinusoid = pos[:, None] * inv_freq[None, :]
            sin = jnp.repeat(jnp.sin(sinusoid) * scale, 2, axis=-1)
            cos = jnp.repeat(jnp.cos(sinusoid) * scale, 2, axis=-1)
            x1 = x[..., ::2]
            x2 = x[..., 1::2]
            rot = jnp.stack([-x2, x1], axis=-1).reshape(x.shape)
            return x * cos + rot * sin

        def _decay_mask(S, gammas):
            n = jnp.arange(S)[:, None]
            m = jnp.arange(S)[None, :]
            diff = (n - m).astype(jnp.float32)
            mask = n >= m
            pw = jnp.maximum(diff, 0.0)[None, :, :]
            return jnp.where(mask[None, :, :], gammas[:, None, None] ** pw, 0.0)

        def retention_forward(Q, K, V):
            B, S, _ = Q.shape

            def split(x, hd):
                return x.reshape(B, S, HEADS, hd).transpose(0, 2, 1, 3)
            q = _xpos(split(Q, HEAD), downscale=False)
            k = _xpos(split(K, HEAD), downscale=True)
            v = split(V, HEAD)
            D = _decay_mask(S, _gammas(HEADS).astype(Q.dtype))
            scores = jnp.einsum('bhsd,bhtd->bhst', q, k) * D[None]
            out = jnp.einsum('bhst,bhtd->bhsd', scores, v)
            return out.transpose(0, 2, 1, 3).reshape(B, S, HEADS * HEAD)
        key = jax.random.key(seed)
        kq, kk, kv = jax.random.split(key, 3)
        B, S = (2, 256)
        return {'Q': jax.random.normal(kq, (B, S, HIDDEN), dtype=jnp.float32), 'K': jax.random.normal(kk, (B, S, HIDDEN), dtype=jnp.float32), 'V': jax.random.normal(kv, (B, S, HIDDEN), dtype=jnp.float32)}
    _L0_xattn_all = _L0_xattn_setup()
    _L0_xattn_in = {k: v for k, v in _L0_xattn_all.items() if k in ()}
    del _L0_xattn_all

    def _L0_ffn_setup():
        import jax, jax.numpy as jnp
        import numpy as np
        W_SCALE = 0.02
        TOP_K = 2
        key = jax.random.key(seed)
        ks = jax.random.split(key, 5)
        B, S, H, I, E = (2, 128, 128, 512, 8)
        return {'x': jax.random.normal(ks[0], (B, S, H), dtype=jnp.float32), 'gate': jax.random.normal(ks[1], (H, E), dtype=jnp.float32) * W_SCALE, 'experts_w1': jax.random.normal(ks[2], (E, H, I), dtype=jnp.float32) * W_SCALE, 'experts_w2': jax.random.normal(ks[3], (E, I, H), dtype=jnp.float32) * W_SCALE, 'experts_w3': jax.random.normal(ks[4], (E, H, I), dtype=jnp.float32) * W_SCALE}
    _L0_ffn_all = _L0_ffn_setup()
    _L0_ffn_in = {k: v for k, v in _L0_ffn_all.items() if k in ('gate', 'experts_w1', 'experts_w2', 'experts_w3')}
    del _L0_ffn_all
    return {'x': x, 'ctx_1024': ctx_1024, 'L0_attn_Wq': _L0_attn_in['Wq'], 'L0_attn_Wk': _L0_attn_in['Wk'], 'L0_attn_Wv': _L0_attn_in['Wv'], 'L0_attn_Wo': _L0_attn_in['Wo'], 'L0_attn_bo': _L0_attn_in['bo'], 'L0_ffn_gate': _L0_ffn_in['gate'], 'L0_ffn_experts_w1': _L0_ffn_in['experts_w1'], 'L0_ffn_experts_w2': _L0_ffn_in['experts_w2'], 'L0_ffn_experts_w3': _L0_ffn_in['experts_w3']}

def reference(x, ctx_1024, L0_attn_Wq, L0_attn_Wk, L0_attn_Wv, L0_attn_Wo, L0_attn_bo, L0_ffn_gate, L0_ffn_experts_w1, L0_ffn_experts_w2, L0_ffn_experts_w3):
    import jax
    import jax.numpy as jnp

    def _L0_attn_ref(x, Wq, Wk, Wv, Wo, bo):
        import jax, jax.numpy as jnp
        import numpy as np
        N_HEADS = 16
        N, S, D = x.shape
        H = N_HEADS
        hd = D // H
        q = (x @ Wq.T).reshape(N, S, H, hd).transpose(0, 2, 1, 3)
        k = (x @ Wk.T).reshape(N, S, H, hd).transpose(0, 2, 1, 3)
        v = (x @ Wv.T).reshape(N, S, H, hd).transpose(0, 2, 1, 3)
        att = jnp.einsum('nqhd,nkhd->nhqk', q, k)
        att = jax.nn.softmax(att / jnp.sqrt(jnp.asarray(hd, x.dtype)), axis=3)
        out = jnp.einsum('nhqk,nkhd->nqhd', att, v).reshape(N, S, D)
        return out @ Wo.T + bo

    def _L0_xattn_ref(Q, K, V):
        import jax, jax.numpy as jnp
        import numpy as np
        import math
        HIDDEN = 128
        HEADS = 16
        HEAD = HIDDEN // HEADS
        SCALE_BASE = 512.0

        def _gammas(heads):
            return 1.0 - jnp.exp(jnp.linspace(math.log(1.0 / 32.0), math.log(1.0 / 512.0), heads))

        def _xpos(x, downscale):
            S, d = (x.shape[2], x.shape[3])
            half = d // 2
            base_scale = (jnp.arange(0, d, 2, dtype=jnp.float32) + 0.4 * d) / (1.4 * d)
            pos = jnp.arange(S, dtype=jnp.float32)
            scale = base_scale[None, :] ** (pos / SCALE_BASE)[:, None]
            if downscale:
                scale = 1.0 / scale
            inv_freq = 1.0 / 10000.0 ** (jnp.arange(half, dtype=jnp.float32) / half)
            sinusoid = pos[:, None] * inv_freq[None, :]
            sin = jnp.repeat(jnp.sin(sinusoid) * scale, 2, axis=-1)
            cos = jnp.repeat(jnp.cos(sinusoid) * scale, 2, axis=-1)
            x1 = x[..., ::2]
            x2 = x[..., 1::2]
            rot = jnp.stack([-x2, x1], axis=-1).reshape(x.shape)
            return x * cos + rot * sin

        def _decay_mask(S, gammas):
            n = jnp.arange(S)[:, None]
            m = jnp.arange(S)[None, :]
            diff = (n - m).astype(jnp.float32)
            mask = n >= m
            pw = jnp.maximum(diff, 0.0)[None, :, :]
            return jnp.where(mask[None, :, :], gammas[:, None, None] ** pw, 0.0)

        def retention_forward(Q, K, V):
            B, S, _ = Q.shape

            def split(x, hd):
                return x.reshape(B, S, HEADS, hd).transpose(0, 2, 1, 3)
            q = _xpos(split(Q, HEAD), downscale=False)
            k = _xpos(split(K, HEAD), downscale=True)
            v = split(V, HEAD)
            D = _decay_mask(S, _gammas(HEADS).astype(Q.dtype))
            scores = jnp.einsum('bhsd,bhtd->bhst', q, k) * D[None]
            out = jnp.einsum('bhst,bhtd->bhsd', scores, v)
            return out.transpose(0, 2, 1, 3).reshape(B, S, HEADS * HEAD)
        return retention_forward(Q, K, V)

    def _L0_ffn_ref(x, gate, experts_w1, experts_w2, experts_w3):
        import jax, jax.numpy as jnp
        import numpy as np
        W_SCALE = 0.02
        TOP_K = 2
        E = experts_w1.shape[0]
        router_logits = jnp.einsum('bsh,he->bse', x, gate)
        routing_weights, selected = jax.lax.top_k(router_logits, TOP_K)
        routing_weights = jax.nn.softmax(routing_weights, axis=-1)
        onehot = jax.nn.one_hot(selected, E, dtype=x.dtype)
        tok_w = jnp.einsum('bsk,bske->bse', routing_weights, onehot)
        g = jnp.einsum('bsh,ehi->ebsi', x, experts_w1)
        u = jnp.einsum('bsh,ehi->ebsi', x, experts_w3)
        hid = jax.nn.silu(g) * u
        eo = jnp.einsum('ebsi,eih->ebsh', hid, experts_w2)
        out = jnp.einsum('ebsh,bse->bsh', eo, tok_w)
        return out
    x = _layernorm(x + _L0_attn_ref(x, L0_attn_Wq, L0_attn_Wk, L0_attn_Wv, L0_attn_Wo, L0_attn_bo), axis=-1)
    x = _layernorm(x + _L0_xattn_ref(x, ctx_1024, ctx_1024), axis=-1)
    x = _layernorm(x + _L0_ffn_ref(x, L0_ffn_gate, L0_ffn_experts_w1, L0_ffn_experts_w2, L0_ffn_experts_w3), axis=-1)
    return x

_drawn_inputs = setup_inputs


def setup_inputs(seed=0):
    import zlib

    import numpy as np

    out = dict(_drawn_inputs(seed))
    spreads = {'L0_attn_bo': (0.0, 0.1)}
    factors = {'L0_attn_Wq': 8.0,
     'L0_attn_Wk': 8.0,
     'L0_attn_Wv': 4.431,
     'L0_attn_Wo': 4.317,
     'L0_ffn_gate': 7.813,
     'L0_ffn_experts_w1': 6.871,
     'L0_ffn_experts_w2': 6.842,
     'L0_ffn_experts_w3': 6.838}
    for name, (base, spread) in spreads.items():
        noise = np.random.default_rng([zlib.crc32(name.encode()), seed]).standard_normal(out[name].shape)
        drawn = base * np.exp(spread * noise) if base else spread * noise
        out[name] = jnp.asarray(drawn.astype(out[name].dtype))
    for name, factor in factors.items():
        out[name] = (out[name] * factor).astype(out[name].dtype)
    return out
```

```python
from contextlib import ExitStack

import numpy as np

import concourse.bass as bass
from concourse import mybir
from concourse.alu_op_type import AluOpType as ALU

ACT = mybir.ActivationFunctionType
AX = mybir.AxisListType
F32 = mybir.dt.float32
BF16 = mybir.dt.bfloat16
I32 = mybir.dt.int32
U32 = mybir.dt.uint32

P = 128
S = 64
NH = 16
HD = 8
UNROLL = 4
RING = 4
ROW = P + 2
EPS = 1e-5


def constants(n_tok, n_exp):
    p = np.arange(P)
    b, t = p // S, p % S
    d = np.arange(P)
    head, r = d // HD, d % HD
    e = r // 2
    gam = 1.0 - np.exp(np.linspace(np.log(1.0 / 32.0), np.log(1.0 / 512.0), P // HD))
    base = (2.0 * np.arange(HD // 2) + 0.4 * HD) / (1.4 * HD)
    inv = 1.0 / 10000.0 ** (np.arange(HD // 2) / (HD // 2))
    ang = t[:, None] * inv[e][None, :]
    scale = base[e][None, :] ** (t[:, None] / 512.0)
    decay = gam[head][None, :] ** t[:, None]
    sign = np.where(r % 2 == 0, -1.0, 1.0)[None, :]
    same = b[:, None] == b[None, :]
    parts = {
        "ident": np.eye(P),
        "tri": same & (t[:, None] <= t[None, :]),
        "before": p[:, None] < p[None, :],
        "group": p[:, None] // NH == np.arange(P // NH),
        "cq": np.cos(ang) * scale * decay,
        "sq": np.sin(ang) * scale * decay * sign,
        "ck": np.cos(ang) / scale / decay,
        "sk": np.sin(ang) / scale / decay * sign,
        "iota_e": np.broadcast_to(np.arange(n_exp), (P, n_exp)),
        "base_e": np.broadcast_to(np.arange(n_exp) * (n_tok + P), (P, n_exp)),
        "lane": p[:, None],
        "spare_id": (n_tok + p)[:, None],
        "ids": p[:, None] + P * np.arange(n_tok // P)[None, :],
        "tile_no": np.broadcast_to(np.arange(2 * n_tok // P + n_exp), (P, 2 * n_tok // P + n_exp)),
    }
    where, at = {}, 0
    for name, a in parts.items():
        n = int(np.prod(a.shape[1:]))
        where[name] = (at, at + n)
        at += n
    table = np.concatenate([np.asarray(a, np.float64).reshape(P, -1) for a in parts.values()], 1)
    return table.astype(np.float32), where


class Item:

    def __init__(self, eng, i, snaps, off):
        self.eng, self.i, self.snaps, self.off = eng, i, snaps, off

    def slot(self, n):
        return self.off % n

    def number(self, lo=0, hi=None):
        return self.off if self.i is None else self.i * UNROLL + self.off

    def count(self, back=0):
        n = self.off + 1 - back
        if self.i is None:
            return n
        key = (UNROLL, n)
        if key not in self.snaps:
            self.snaps[key] = self.eng.snap(self.i * UNROLL + n)
        return self.snaps[key]

    def ring_count(self, per, back=0):
        n = (self.off - back) // RING + 1
        if self.i is None:
            return per * n
        key = (per, n)
        if key not in self.snaps:
            self.snaps[key] = self.eng.snap((self.i + n) * per)
        return self.snaps[key]


def wait(item, sem, back=0):
    if item.i is None and item.off + 1 - back <= 0:
        return
    item.eng.wait_ge(sem, item.count(back))


def wait_ring(item, sems, back=0, per=16):
    if item.i is None and item.off - back < 0:
        return
    item.eng.wait_ge(sems[(item.off - back) % RING], item.ring_count(per, back))


def run_steps(eng, n, first, lags, body):
    def alone(s):
        body(lambda lag: Item(eng, None, None, s - lag) if 0 <= s - lag < n else None)

    for s in range(first):
        alone(s)
    if n > first:
        with eng.Fori(0, (n - first) // UNROLL) as i:
            snaps = {}
            for k in range(UNROLL):
                body(lambda lag, k=k: Item(eng, i, snaps, first + k - lag))
    for s in range(n, n + lags):
        alone(s)


def build(nc, x, ctx, w_qkv, wo_by_token, bo, gate, w1, w3, w2, table, where, out):
    n_tok = x.shape[0]
    n_exp, inner = w1.shape[0], w1.shape[2]
    n_chunk = inner // P
    n_duo = n_tok // (2 * P)
    region = n_tok + P
    n_tiles = 2 * n_tok // P + n_exp
    A_FIRST, A_LAGS = 12, 5
    B_FIRST, B_LAGS = 4, 3
    C_SLICES = 4
    n_chunks_c = n_tok // P // C_SLICES
    C_FIRST, C_LAGS = 4, 1
    assert (n_duo - A_FIRST) % UNROLL == 0 and (n_tiles - B_FIRST) % UNROLL == 0

    xs = nc.dram_tensor("routed_rows", [n_exp * region + P, ROW], F32).ap()
    acc = nc.dram_tensor("residual_sum", [n_tok + P, P], F32).ap()

    x_duos = x.rearrange("(n u p) d -> n p u d", u=2, p=P)
    ctx_duos = ctx.rearrange("(n u p) d -> n p u d", u=2, p=P)
    acc_duos = acc[0:n_tok, :].rearrange("(n u p) d -> n p u d", u=2, p=P)
    acc_rows = acc[0:n_tok, :].rearrange("(p n) d -> p n d", p=P)
    out_rows = out.rearrange("(p n) d -> p n d", p=P)

    with ExitStack() as stack:
        def sb(name, shape, dt=F32):
            return stack.enter_context(nc.sbuf_tensor(name, [P, *shape], dt))

        def ps(name, n):
            return stack.enter_context(nc.psum_tensor(name, [P, n], F32))

        def sem(name):
            return stack.enter_context(nc.semaphore(name))

        def ring_sem(name):
            return [sem(f"{name}{i}") for i in range(RING)]

        tab = sb("tab", [table.shape[1]])

        def const(name):
            a, b = where[name]
            return tab[:, a:b]

        ident, tri = const("ident"), const("tri")
        w_qkv_sb = sb("w_qkv_sb", [3 * P])
        wo_sb = sb("wo_sb", [HD, P])
        bo_sb = sb("bo_sb", [1])
        gate_sb = sb("gate_sb", [n_exp])
        w1_sb = sb("w1_sb", [n_exp * inner])
        w3_sb = sb("w3_sb", [n_exp * inner])
        w2_sb = sb("w2_sb", [n_exp * inner])
        before_bf = sb("before_bf", [P], BF16)
        ones_bf = sb("ones_bf", [P], BF16)
        eps_c = sb("eps_c", [8])
        half_c = sb("half_c", [8])
        pad_rows = sb("pad_rows", [ROW])

        x_sb, ctx_sb = sb("x_sb", [RING, 2, P]), sb("ctx_sb", [RING, 2, P])
        x_t = sb("x_t", [2, 2, P])
        qkv = sb("qkv", [2, 2, 3 * P])
        prod_qk = sb("prod_qk", [2, HD, NH * NH])
        m_sb = sb("m_sb", [2, NH])
        s_m = sb("s_m", [2, NH * NH])
        e_sb = sb("e_sb", [2, 2, NH * NH])
        den, r_den = sb("den", [2, NH]), sb("r_den", [2, 2, NH])
        prod_ev = sb("prod_ev", [2, NH, HD, NH])
        o_raw = sb("o_raw", [2, P])
        o_n = sb("o_n", [2, 2, HD, NH])
        o_g = sb("o_g", [2, HD, HD, NH])
        y_t = sb("y_t", [2, P])
        res1, res2 = sb("res1", [2, 2, P]), sb("res2", [2, 2, P])
        stat1, stat2 = sb("stat1", [2, 2, 6]), sb("stat2", [2, 2, 6])
        mv1, mv2 = sb("mv1", [2, 2, 2]), sb("mv2", [2, 2, 2])
        ve1, ve2 = sb("ve1", [2, 2]), sb("ve2", [2, 2])
        rs1, rs2 = sb("rs1", [2, 2]), sb("rs2", [2, 2])
        x1 = sb("x1", [2, 2, P])
        xq_a, xq_b, xq = sb("xq_a", [2, P]), sb("xq_b", [2, P]), sb("xq", [2, P])
        xk_a, xk_b, xk = sb("xk_a", [2, P]), sb("xk_b", [2, P]), sb("xk", [2, P])
        kv = sb("kv", [2, 2, 1024])
        prod_kv = sb("prod_kv", [2, 1024])
        ret = sb("ret", [2, P])
        xe = sb("xe", [RING, 2, 2, ROW])
        x2_t = sb("x2_t", [2, 2, P])
        lg = sb("lg", [2, 2, n_exp])
        mx8, ix8 = sb("mx8", [2, 2, 8]), sb("ix8", [2, 2, 8], U32)
        dlt, ex, dn = sb("dlt", [2, 2]), sb("ex", [2, 2]), sb("dn", [2, 2])
        oh = sb("oh", [2, 2, 2, n_exp])
        ohs = sb("ohs", [2, 2, n_exp], BF16)
        cnt = sb("cnt", [n_exp])
        posf, posw = sb("posf", [2, n_exp]), sb("posw", [2, 2, n_exp])
        pos = sb("pos", [RING, 4], I32)

        pad_f, pad_i = sb("pad_f", [n_exp]), sb("pad_i", [n_exp], I32)
        c_cnt, c_int, c_sh = sb("c_cnt", [n_exp]), sb("c_int", [n_exp], I32), sb("c_sh", [n_exp], I32)
        n_t, cum = sb("n_t", [n_exp]), sb("cum", [n_exp])
        t_ge, t_exp, t_prev, t_base, t_dif = (sb(n, [n_tiles]) for n in ("t_ge", "t_exp", "t_prev", "t_base", "t_dif"))
        tile_exp, tile_base = sb("tile_exp", [n_tiles], I32), sb("tile_base", [n_tiles], I32)

        xg = sb("xg", [RING, ROW])
        xg_t = sb("xg_t", [2, P])
        sil = sb("sil", [2, inner])
        hid = sb("hid", [2, inner])
        hid_t = sb("hid_t", [2, inner])
        yw = sb("yw", [RING, P])
        tok_i = sb("tok_i", [RING, 1], I32)

        fin = sb("fin", [RING, C_SLICES, P])
        fstat, fmv = sb("fstat", [2, C_SLICES, 6]), sb("fmv", [2, C_SLICES, 2])
        fve, frs = sb("fve", [2, C_SLICES]), sb("frs", [2, C_SLICES])

        XT, SC, YY, TR = ps("XT", 512), ps("SC", 512), ps("YY", 512), ps("TR", 512)
        QKV, KV = ps("QKV", 1024), ps("KV", 1024)
        qkv_ps = QKV[:, :].rearrange("p (u c) -> p u c", u=2)[:, :, 0:3 * P]
        YT, Y = YY[:, 0:2 * P], YY[:, 2 * P:4 * P]
        X2T, LG, RANK = TR[:, 0:2 * P], TR[:, 256:256 + 2 * n_exp], TR[:, 288:288 + 3 * n_exp]

        tab_in, small_in, big_in = sem("tab_in"), sem("small_in"), sem("big_in")
        consts_ready, pool_consts = sem("consts_ready"), sem("pool_consts")
        xt_done, qkv_done, score_done, x2t_done, logit_done, yt_done, y_done, rank_done = (
            sem(n) for n in ("xt_done", "qkv_done", "score_done", "x2t_done", "logit_done", "yt_done", "y_done",
                             "rank_done"))
        kv_done = [sem(f"kv_done{n}") for n in range(4)]
        xt_ready, qkv_ready, e_ready, og_ready, yt_ready, x2t_ready, ex_ready = (
            sem(n) for n in ("xt_ready", "qkv_ready", "e_ready", "og_ready", "yt_ready", "x2t_ready", "ex_ready"))
        qk_ready = [sem(f"qk_ready{u}") for u in range(2)]
        kvp_ready = [sem(f"kvp_ready{n}") for n in range(4)]
        m_ready, sm_ready, den_ready, rden_ready, oraw_ready, on_ready = (
            sem(n) for n in ("m_ready", "sm_ready", "den_ready", "rden_ready", "oraw_ready", "on_ready"))
        lg_ready, mx_ready, ix_ready, oh_ready, ohs_ready, dlt_ready = (
            sem(n) for n in ("lg_ready", "mx_ready", "ix_ready", "oh_ready", "ohs_ready", "dlt_ready"))
        res2_ready, stat2_ready, mv2_ready, res1_ready, stat1_ready, mv1_ready, ret_ready = (
            sem(n) for n in ("res2_ready", "stat2_ready", "mv2_ready", "res1_ready", "stat1_ready", "mv1_ready",
                             "ret_ready"))
        x1_ready, x2_ready, dn_ready, w1_ready, w2_ready = (
            sem(n) for n in ("x1_ready", "x2_ready", "dn_ready", "w1_ready", "w2_ready"))
        xqa_ready, xqb_ready, xq_ready = (sem(n) for n in ("xqa_ready", "xqb_ready", "xq_ready"))
        posf_ready, cnt_ready, posw_ready, pos_ready = (
            sem(n) for n in ("posf_ready", "cnt_ready", "posw_ready", "pos_ready"))
        xka_ready, xkb_ready, xk_ready, kv_ready, id_ready, ev_ready = (
            sem(n) for n in ("xka_ready", "xkb_ready", "xk_ready", "kv_ready", "id_ready", "ev_ready"))
        ve1_ready, rs1_ready, ve2_ready, rs2_ready = (
            sem(n) for n in ("ve1_ready", "rs1_ready", "ve2_ready", "rs2_ready"))
        x_in, ctx_in, acc_out, routed_out = (ring_sem(n) for n in ("x_in", "ctx_in", "acc_out", "routed_out"))
        chain, padi_ready, table_ready, pads_out = sem("chain"), sem("padi_ready"), sem("table_ready"), sem("pads_out")
        spare_out = sem("spare_out")
        xg_in, added = ring_sem("xg_in"), ring_sem("added")
        xgt_done, gu_done, ht_done, down_done = (sem(n) for n in ("xgt_done", "gu_done", "ht_done", "down_done"))
        xgt_ready, sil_ready, ht_ready = (sem(n) for n in ("xgt_ready", "sil_ready", "ht_ready"))
        hid_ready, yw_ready, tok_ready = (sem(n) for n in ("hid_ready", "yw_ready", "tok_ready"))
        fin_in, fin_out = ring_sem("fin_in"), ring_sem("fin_out")
        fstat_ready, fmv_ready, fve_ready, frs_ready, fout_ready = (
            sem(n) for n in ("fstat_ready", "fmv_ready", "fve_ready", "frs_ready", "fout_ready"))

        marks = sb("marks", [6])
        marked = [sem(f"marked{n}") for n in range(6)]

        def stand(it, n):
            wait(it, marked[n], 1)
            if n < 4:
                it.eng.memset(marks[:, n:n + 1], 0.0).then_inc(marked[n], 1)
            else:
                it.eng.tensor_tensor(marks[:, n:n + 1], half_c[:, 0:1], half_c[:, 0:1], ALU.add).then_inc(marked[n], 1)

        def swapped(ap):
            return couples(ap)[:, :, ::-1]

        def couples(ap):
            return ap.rearrange("p (e w) -> p e w", w=2)

        def twice(ap):
            return ap.unsqueeze(1).to_broadcast([P, 2, ap.shape[1]])

        block = stack.enter_context(nc.Block())

        @block.sync
        def _(eng):
            eng.dma_start(tab[:, :], table).then_inc(tab_in, 16)
            eng.dma_start(w_qkv_sb[:, :], w_qkv).then_inc(small_in, 16)
            eng.dma_start(wo_sb[:, :, :], wo_by_token).then_inc(small_in, 16)
            eng.dma_start(bo_sb[:, :], bo).then_inc(small_in, 16)
            eng.dma_start(gate_sb[:, :], gate).then_inc(small_in, 16)
            eng.wait_ge(consts_ready, 1)
            eng.dma_start(acc[n_tok:n_tok + P, :], pad_rows[:, 0:P]).then_inc(spare_out, 16)

            def step(at):
                if z := at(0):
                    wait(z, res1_ready, RING)
                    eng.dma_start(x_sb[:, z.slot(RING), :, :], x_duos[z.number()]).then_inc(x_in[z.slot(RING)], 16)
                    wait(z, kv_ready, RING)
                    eng.dma_start(ctx_sb[:, z.slot(RING), :, :], ctx_duos[z.number()]).then_inc(ctx_in[z.slot(RING)], 16)
                if e := at(5):
                    wait(e, x2_ready)
                    eng.dma_start(acc_duos[e.number()], xe[:, e.slot(RING), :, 0, 0:P]).then_inc(acc_out[e.slot(RING)], 16)

            run_steps(eng, n_duo, A_FIRST, A_LAGS, step)

            for r in range(RING):
                eng.wait_ge(routed_out[r], 64 * n_duo // RING)
                eng.wait_ge(acc_out[r], 16 * n_duo // RING)
            eng.wait_ge(pads_out, 16 * (n_exp + 1))
            eng.wait_ge(spare_out, 16)
            eng.wait_ge(table_ready, 1)

            def load_tile(at):
                if t := at(0):
                    row = eng.value_load(tile_base[0:1, bass.ds(t.number(), 1)], min_val=0, max_val=n_exp * region)
                    wait(t, yw_ready, RING)
                    wait(t, tok_ready, RING)
                    eng.dma_start(xg[:, t.slot(RING), :], xs[bass.ds(row, P), :]).then_inc(xg_in[t.slot(RING)], 16)

            run_steps(eng, n_tiles, B_FIRST, 0, load_tile)

            for r in range(RING):
                eng.wait_ge(added[r], 16 * n_tiles // RING)

            def last_norm(at):
                if c := at(0):
                    wait_ring(c, fin_out, RING)
                    eng.dma_start(fin[:, c.slot(RING), :, :],
                                  acc_rows[:, bass.ds(c.number() * C_SLICES, C_SLICES), :]).then_inc(fin_in[c.slot(RING)], 16)
                if c := at(1):
                    wait(c, fout_ready)
                    eng.dma_start(out_rows[:, bass.ds(c.number() * C_SLICES, C_SLICES), :],
                                  fin[:, c.slot(RING), :, :]).then_inc(fin_out[c.slot(RING)], 16)

            run_steps(eng, n_chunks_c, C_FIRST, C_LAGS, last_norm)
            for r in range(RING):
                eng.wait_ge(fin_out[r], 16 * n_chunks_c // RING)

        @block.tensor
        def _(eng):
            eng.wait_ge(tab_in, 16)
            eng.wait_ge(small_in, 16 * 4)
            eng.wait_ge(consts_ready, 1)

            def step(at):
                z, a, b, c, d = (at(lag) for lag in range(5))
                if z:
                    wait_ring(z, x_in)
                    wait(z, xt_ready, 1)
                    for u in range(2):
                        mm = eng.transpose(XT[:, P * u:P * u + P], x_sb[:, z.slot(RING), u, :], ident)
                    mm.then_inc(xt_done, 1)
                if d:
                    wait(d, x2_ready)
                    wait(d, posf_ready, 1)
                    wait(d, cnt_ready, 1)
                    for u in range(2):
                        mm = eng.transpose(X2T[:, P * u:P * u + P], xe[:, d.slot(RING), u, 0, 0:P], ident)
                    mm.then_inc(x2t_done, 1)
                if z:
                    wait(z, xt_ready)
                    wait(z, qkv_ready, 1)
                    for u in range(2):
                        mm = eng.matmul(qkv_ps[:, u, :], x_t[:, z.slot(2), u, :], w_qkv_sb[:, :], start=True, stop=True)
                    mm.then_inc(qkv_done, 1)
                if a:
                    wait(a, sm_ready, 1)
                    for u in range(2):
                        wait(a, qk_ready[u])
                        for n in range(HD):
                            mm = eng.matmul(SC[:, 256 * u:256 * u + 256], ident, prod_qk[:, u, n, :],
                                            start=(n == 0), stop=(n == HD - 1))
                    mm.then_inc(score_done, 1)
                if d:
                    wait(d, x2t_ready)
                    for u in range(2):
                        mm = eng.matmul(LG[:, n_exp * u:n_exp * u + n_exp], x2_t[:, d.slot(2), u, :], gate_sb[:, :],
                                        start=True, stop=True)
                    mm.then_inc(logit_done, 1)

                def kv_sums(n):
                    if n < 2:
                        wait(c, kvp_ready[n + 2], 1)
                    else:
                        wait(c, kvp_ready[n - 2])
                    eng.matmul(KV[:, 512 * (n % 2):512 * (n % 2) + 512], tri,
                               kv[:, c.slot(2), n // 2, 512 * (n % 2):512 * (n % 2) + 512],
                               start=True, stop=True).then_inc(kv_done[n], 1)

                if c:
                    wait(c, kv_ready)
                    kv_sums(0)
                    kv_sums(1)
                if b:
                    wait(b, og_ready)
                    wait(b, res1_ready, 1)
                    for n in range(HD):
                        mm = eng.matmul(YT, wo_sb[:, n, :], o_g[:, :, n, :, :].rearrange("p u g h -> p u (g h)"),
                                        start=(n == 0), stop=(n == HD - 1))
                    mm.then_inc(yt_done, 1)
                if c:
                    kv_sums(2)
                    kv_sums(3)
                if b:
                    wait(b, yt_ready)
                    for u in range(2):
                        mm = eng.transpose(Y[:, P * u:P * u + P], y_t[:, u, :], ident)
                    mm.then_inc(y_done, 1)
                if d:
                    wait(d, ohs_ready)
                    o = ohs[:, d.slot(2), :, :]
                    eng.matmul(RANK[:, 0:2 * n_exp], before_bf[:, :], o.rearrange("p u e -> p (u e)"),
                               start=True, stop=False, skip_group_check=True)
                    eng.matmul(RANK[:, n_exp:2 * n_exp], ones_bf[:, :], o[:, 0, :], start=False, stop=True,
                               skip_group_check=True)
                    for u in range(2):
                        mm = eng.matmul(RANK[:, 2 * n_exp:3 * n_exp], ones_bf[:, :], o[:, u, :],
                                        start=(u == 0), stop=(u == 1), skip_group_check=True)
                    mm.then_inc(rank_done, 1)

            run_steps(eng, n_duo, A_FIRST, A_LAGS, step)

            eng.wait_ge(big_in, 16 * (2 + n_chunk))
            eng.wait_ge(table_ready, 1)
            eng.wait_ge(pos_ready, n_duo)
            G = [QKV[:, 0:512], QKV[:, 512:1024]]
            U = [KV[:, 0:512], KV[:, 512:1024]]
            HT = [XT, SC]

            def tile_step(at):
                if t := at(0):
                    wait_ring(t, xg_in)
                    wait(t, xgt_ready, 1)
                    eng.transpose(TR[:, 0:P], xg[:, t.slot(RING), 0:P], ident).then_inc(xgt_done, 1)
                if t := at(2):
                    wait(t, hid_ready)
                    wait(t, ht_ready, 2)
                    for n in range(n_chunk):
                        mm = eng.transpose(HT[t.slot(2)][:, P * n:P * n + P], hid[:, t.slot(2), P * n:P * n + P], ident)
                    mm.then_inc(ht_done, 1)
                if t := at(1):
                    ex_no = eng.value_load(tile_exp[0:1, bass.ds(t.number(), 1)], min_val=0, max_val=n_exp - 1)
                    wait(t, xgt_ready)
                    wait(t, sil_ready, 2)
                    wait(t, hid_ready, 2)
                    cols = bass.ds(ex_no * inner, inner)
                    eng.matmul(G[t.slot(2)], xg_t[:, t.slot(2), :], w1_sb[:, cols], start=True, stop=True)
                    eng.matmul(U[t.slot(2)], xg_t[:, t.slot(2), :], w3_sb[:, cols],
                               start=True, stop=True).then_inc(gu_done, 1)
                if t := at(2):
                    ex_no = eng.value_load(tile_exp[0:1, bass.ds(t.number(), 1)], min_val=0, max_val=n_exp - 1)
                    wait(t, ht_ready)
                    wait(t, yw_ready, 1)
                    for n in range(n_chunk):
                        mm = eng.matmul(YY[:, 0:P], hid_t[:, t.slot(2), P * n:P * n + P],
                                        w2_sb[:, bass.ds(ex_no * inner + P * n, P)],
                                        start=(n == 0), stop=(n == n_chunk - 1))
                    mm.then_inc(down_done, 1)

            run_steps(eng, n_tiles, B_FIRST, B_LAGS, tile_step)

        @block.scalar
        def _(eng):
            eng.dma_start(w1_sb[:, :].rearrange("p (e i) -> p e i", e=n_exp), w1.rearrange("e h i -> h e i")).then_inc(big_in, 16)
            eng.dma_start(w3_sb[:, :].rearrange("p (e i) -> p e i", e=n_exp), w3.rearrange("e h i -> h e i")).then_inc(big_in, 16)
            w2_v = w2.rearrange("e (n p) h -> n p e h", p=P)
            w2_s = w2_sb[:, :].rearrange("p (e n h) -> p e n h", e=n_exp, n=n_chunk)
            for n in range(n_chunk):
                eng.dma_start(w2_s[:, :, n, :], w2_v[n]).then_inc(big_in, 16)
            eng.wait_ge(tab_in, 16)
            eng.wait_ge(small_in, 16 * 4)

            def step(at):
                z, a, b, d = (at(lag) for lag in (0, 1, 2, 4))
                if z:
                    wait(z, xt_done)
                    wait(z, qkv_done, 2)
                    eng.copy(x_t[:, z.slot(2), :, :].rearrange("p u t -> p (u t)"), XT[:, 0:2 * P]).then_inc(xt_ready, 1)
                if d:
                    wait(d, x2t_done)
                    wait(d, logit_done, 2)
                    eng.copy(x2_t[:, d.slot(2), :, :].rearrange("p u t -> p (u t)"), X2T).then_inc(x2t_ready, 1)
                if z:
                    wait(z, qkv_done)
                    wait(z, ev_ready, 2)
                    wait(z, qk_ready[1], 2)
                    eng.copy(qkv[:, z.slot(2), :, :], qkv_ps).then_inc(qkv_ready, 1)
                if b:
                    wait(b, on_ready)
                    wait(b, yt_done, 1)
                    for g in range(P // NH):
                        ins = eng.activation(o_g[:, :, :, g, :], o_n[:, b.slot(2), :, :, :], ACT.Copy,
                                             scale=const("group")[:, g:g + 1])
                    ins.then_inc(og_ready, 1)
                if a:
                    wait(a, sm_ready)
                    wait(a, ev_ready, 2)
                    wait(a, den_ready, 2)
                    eng.activation(e_sb[:, a.slot(2), :, :], s_m[:, :, :], ACT.Exp, scale=float(HD) ** -0.5).then_inc(e_ready, 1)
                if d:
                    wait(d, dlt_ready)
                    wait(d, w2_ready, 2)
                    eng.activation(ex[:, d.slot(2), :], dlt[:, d.slot(2), :], ACT.Exp).then_inc(ex_ready, 1)
                if b:
                    wait(b, yt_done)
                    wait(b, y_done, 1)
                    for u in range(2):
                        ins = eng.activation(y_t[:, u, :].rearrange("p (b h g) -> p b g h", b=2, h=NH),
                                             YT[:, P * u:P * u + P].rearrange("p (b g h) -> p b g h", b=2, h=NH),
                                             ACT.Identity, bias=bo_sb[:, :])
                    ins.then_inc(yt_ready, 1)

            run_steps(eng, n_duo, A_FIRST, A_LAGS, step)

            G = [QKV[:, 0:512], QKV[:, 512:1024]]
            HT = [XT, SC]

            def tile_step(at):
                if t := at(0):
                    wait(t, xgt_done)
                    wait(t, gu_done, 2)
                    eng.copy(xg_t[:, t.slot(2), :], TR[:, 0:P]).then_inc(xgt_ready, 1)
                if t := at(2):
                    wait(t, ht_done)
                    wait(t, down_done, 2)
                    eng.copy(hid_t[:, t.slot(2), :], HT[t.slot(2)][:, :]).then_inc(ht_ready, 1)
                if t := at(1):
                    wait(t, gu_done)
                    wait(t, hid_ready, 2)
                    eng.activation(sil[:, t.slot(2), :], G[t.slot(2)], ACT.Silu).then_inc(sil_ready, 1)

            run_steps(eng, n_tiles, B_FIRST, B_LAGS, tile_step)

        @block.vector
        def _(eng):
            eng.memset(ones_bf[:, :], 1.0)
            eng.memset(pad_rows[:, 0:P + 1], 0.0)
            eng.wait_ge(tab_in, 16)
            eng.tensor_copy(pad_rows[:, P + 1:ROW], const("spare_id"))
            eng.tensor_copy(before_bf[:, :], const("before"))
            eng.tensor_copy(cnt[:, :], const("base_e")).then_inc(consts_ready, 1)
            eng.wait_ge(consts_ready, 1)

            def statistics(it, mark, res, stat, mv, res_ready, stat_ready, mv_ready, used):
                s = it.slot(2)
                wait(it, res_ready)
                wait(it, mv_ready, 2)
                for u in range(2):
                    ins = eng.bn_stats(stat[:, s, u, :], res[:, s, u, :])
                ins.then_inc(stat_ready, 1)
                wait(it, stat_ready)
                wait(it, used, 2)
                stand(it, mark)
                for u in range(2):
                    ins = eng.bn_aggr(mv[:, s, u, :], stat[:, s, u, :])
                ins.then_inc(mv_ready, 1)

            def step(at):
                a, b, c, d = (at(lag) for lag in (1, 2, 3, 4))
                if a:
                    s = a.slot(2)
                    wait(a, qkv_ready)
                    wait(a, score_done, 1)
                    for u in range(2):
                        q = qkv[:, s, u, 0:P].rearrange("p (d i) -> p d i", i=NH)
                        k = qkv[:, s, u, P:2 * P].rearrange("p (d j) -> p d j", j=NH)
                        eng.tensor_tensor(prod_qk[:, u, :, :].rearrange("p d (i j) -> p d i j", j=NH),
                                          q.unsqueeze(3).to_broadcast([P, HD, NH, NH]),
                                          k.unsqueeze(2).to_broadcast([P, HD, NH, NH]), ALU.mult).then_inc(qk_ready[u], 1)
                if c:
                    s = c.slot(2)
                    wait(c, rs1_ready)
                    wait(c, res2_ready, 2)
                    for u in range(2):
                        ins = eng.tensor_scalar(x1[:, s, u, :], res1[:, s, u, :], mv1[:, s, u, 0:1], rs1[:, s, u:u + 1],
                                                ALU.subtract, ALU.mult)
                    ins.then_inc(x1_ready, 1)
                if d:
                    s = d.slot(2)
                    wait(d, rs2_ready)
                    wait_ring(d, routed_out, RING, 64)
                    wait_ring(d, acc_out, RING)
                    wait(d, x2t_done, RING)
                    for u in range(2):
                        ins = eng.tensor_scalar(xe[:, d.slot(RING), u, :, 0:P],
                                                res2[:, s, u, :].unsqueeze(1).to_broadcast([P, 2, P]),
                                                mv2[:, s, u, 0:1], rs2[:, s, u:u + 1], ALU.subtract, ALU.mult)
                    ins.then_inc(x2_ready, 1)
                if c:
                    s = c.slot(2)
                    wait(c, x1_ready)
                    wait(c, xq_ready, 1)
                    eng.tensor_tensor(xq_a[:, :, :], x1[:, s, :, :], twice(const("cq")), ALU.mult).then_inc(xqa_ready, 1)
                    for u in range(2):
                        ins = eng.tensor_tensor(couples(xq_b[:, u, :]), swapped(x1[:, s, u, :]), couples(const("sq")), ALU.mult)
                    ins.then_inc(xqb_ready, 1)
                    wait(c, xqa_ready)
                    wait(c, xqb_ready)
                    wait(c, kvp_ready[3], 1)
                    eng.tensor_tensor(xq[:, :, :], xq_a[:, :, :], xq_b[:, :, :], ALU.add).then_inc(xq_ready, 1)
                if b:
                    s = b.slot(2)
                    wait(b, ev_ready)
                    wait(b, on_ready, 1)
                    for u in range(2):
                        ins = eng.tensor_reduce(o_raw[:, u, :], prod_ev[:, u, :, :, :], AX.X, ALU.add)
                    ins.then_inc(oraw_ready, 1)
                    wait(b, oraw_ready)
                    wait(b, rden_ready)
                    wait(b, og_ready, 2)
                    for u in range(2):
                        ins = eng.tensor_tensor(o_n[:, s, u, :, :].rearrange("p d i -> p i d"),
                                                o_raw[:, u, :].rearrange("p (i d) -> p i d", d=HD),
                                                r_den[:, s, u, :].unsqueeze(2).to_broadcast([P, NH, HD]), ALU.mult)
                    ins.then_inc(on_ready, 1)
                if a:
                    wait(a, score_done)
                    wait(a, sm_ready, 1)
                    sc = SC[:, :].rearrange("p (u i j) -> p (u i) j", u=2, j=NH)
                    eng.tensor_reduce(m_sb[:, :, :].rearrange("p u i -> p (u i)"), sc, AX.X, ALU.max).then_inc(m_ready, 1)
                    wait(a, m_ready)
                    wait(a, e_ready, 1)
                    eng.tensor_tensor(s_m[:, :, :].rearrange("p u (i j) -> p (u i) j", j=NH), sc,
                                      m_sb[:, :, :].rearrange("p u i -> p (u i)").unsqueeze(2).to_broadcast([P, 2 * NH, NH]),
                                      ALU.subtract).then_inc(sm_ready, 1)
                if c:
                    wait(c, xq_ready)
                    wait(c, ret_ready, 1)
                    for n in range(4):
                        u, h0 = n // 2, 8 * (n % 2)
                        wait(c, kv_done[n])
                        qv = xq[:, u, :].rearrange("p (h i) -> p h i", i=HD)[:, h0:h0 + 8, :]
                        eng.tensor_tensor(
                            prod_kv[:, u, 64 * h0:64 * h0 + 512].rearrange("p (h j i) -> p h j i", j=HD, i=HD),
                            KV[:, 512 * (n % 2):512 * (n % 2) + 512].rearrange("p (h j i) -> p h j i", j=HD, i=HD),
                            qv.unsqueeze(2).to_broadcast([P, 8, HD, HD]), ALU.mult).then_inc(kvp_ready[n], 1)
                    for n in range(4):
                        wait(c, kvp_ready[n])
                    wait(c, res2_ready, 1)
                    eng.tensor_reduce(ret[:, :, :].rearrange("p u d -> p (u d)"),
                                      prod_kv[:, :, :].rearrange("p u (d i) -> p (u d) i", i=HD), AX.X,
                                      ALU.add).then_inc(ret_ready, 1)
                if d:
                    s = d.slot(2)
                    wait(d, logit_done)
                    wait(d, ix_ready, 2)
                    eng.tensor_copy(lg[:, s, :, :].rearrange("p u e -> p (u e)"), LG).then_inc(lg_ready, 1)
                    wait(d, lg_ready)
                    wait(d, dlt_ready, 2)
                    stand(d, 2)
                    for u in range(2):
                        ins = eng.max(mx8[:, s, u, :], lg[:, s, u, :])
                    ins.then_inc(mx_ready, 1)
                    wait(d, mx_ready)
                    wait(d, ex_ready, 2)
                    eng.tensor_tensor(dlt[:, s, :], mx8[:, s, :, 1], mx8[:, s, :, 0], ALU.subtract).then_inc(dlt_ready, 1)
                    for u in range(2):
                        ins = eng.max_index(ix8[:, s, u, :], mx8[:, s, u, :], lg[:, s, u, :])
                    ins.then_inc(ix_ready, 1)
                if c:
                    s = c.slot(2)
                    wait(c, ret_ready)
                    wait(c, x2_ready, 2)
                    eng.tensor_tensor(res2[:, s, :, :], ret[:, :, :], x1[:, s, :, :], ALU.add).then_inc(res2_ready, 1)
                    statistics(c, 1, res2, stat2, mv2, res2_ready, stat2_ready, mv2_ready, x2_ready)
                if d:
                    s = d.slot(2)
                    wait(d, ix_ready)
                    wait(d, posw_ready, 2)
                    for u in range(2):
                        ins = eng.tensor_tensor(oh[:, s, u, :, :], twice(const("iota_e")),
                                                ix8[:, s, u, 0:2].unsqueeze(2).to_broadcast([P, 2, n_exp]), ALU.is_equal)
                    ins.then_inc(oh_ready, 1)
                    wait(d, oh_ready)
                    wait(d, rank_done, 2)
                    eng.tensor_tensor(ohs[:, s, :, :], oh[:, s, :, 0, :], oh[:, s, :, 1, :], ALU.add).then_inc(ohs_ready, 1)
                if a:
                    s = a.slot(2)
                    wait(a, e_ready)
                    wait(a, rden_ready, 1)
                    eng.tensor_reduce(den[:, :, :].rearrange("p u i -> p (u i)"),
                                      e_sb[:, s, :, :].rearrange("p u (i j) -> p (u i) j", j=NH), AX.X,
                                      ALU.add).then_inc(den_ready, 1)
                    wait(a, den_ready)
                    wait(a, on_ready, 2)
                    eng.reciprocal(r_den[:, s, :, :], den[:, :, :]).then_inc(rden_ready, 1)
                if d:
                    s, r = d.slot(2), d.slot(RING)
                    wait(d, ex_ready)
                    wait(d, w1_ready, 2)
                    eng.tensor_scalar(dn[:, s, :], ex[:, s, :], 1.0, None, ALU.add).then_inc(dn_ready, 1)
                    wait(d, dn_ready)
                    eng.reciprocal(xe[:, r, :, 0, P], dn[:, s, :]).then_inc(w1_ready, 1)
                    wait(d, w1_ready)
                    eng.tensor_tensor(xe[:, r, :, 1, P], ex[:, s, :], xe[:, r, :, 0, P], ALU.mult).then_inc(w2_ready, 1)
                if b:
                    s = b.slot(2)
                    wait(b, y_done)
                    wait(b, x1_ready, 2)
                    eng.tensor_tensor(res1[:, s, :, :], Y.rearrange("p (u c) -> p u c", u=2), x_sb[:, b.slot(RING), :, :],
                                      ALU.add).then_inc(res1_ready, 1)
                    statistics(b, 0, res1, stat1, mv1, res1_ready, stat1_ready, mv1_ready, x1_ready)
                if d:
                    s = d.slot(2)
                    wait(d, rank_done)
                    wait(d, cnt_ready, 1)
                    wait(d, posw_ready, 1)
                    eng.tensor_tensor(posf[:, :, :], RANK[:, 0:2 * n_exp].rearrange("p (u e) -> p u e", u=2),
                                      twice(cnt[:, :]), ALU.add).then_inc(posf_ready, 1)
                    wait(d, posf_ready)
                    eng.tensor_tensor(cnt[:, :], RANK[:, 2 * n_exp:3 * n_exp], cnt[:, :], ALU.add).then_inc(cnt_ready, 1)
                    wait(d, pos_ready, 1)
                    eng.tensor_tensor(posw[:, :, :, :], oh[:, s, :, :, :],
                                      posf[:, :, :].unsqueeze(2).to_broadcast([P, 2, 2, n_exp]), ALU.mult).then_inc(posw_ready, 1)
                    wait(d, posw_ready)
                    wait_ring(d, routed_out, RING, 64)
                    with nc.allow_low_precision(reason="whole numbers below 2**24"):
                        eng.tensor_reduce(pos[:, d.slot(RING), :], posw[:, :, :, :].rearrange("p u k e -> p (u k) e"),
                                          AX.X, ALU.add).then_inc(pos_ready, 1)

            run_steps(eng, n_duo, A_FIRST, A_LAGS, step)

            links = [0]

            def link(ins):
                links[0] += 1
                ins.then_inc(chain, 1)
                eng.wait_ge(chain, links[0])

            eng.wait_ge(cnt_ready, n_duo)
            link(eng.tensor_scalar(pad_f[:, :], cnt[:, :], const("lane"), None, ALU.add))
            eng.tensor_copy(pad_i[:, :], pad_f[:, :]).then_inc(padi_ready, 1)
            one = slice(0, 1)
            link(eng.tensor_tensor(c_cnt[one, :], cnt[one, :], const("base_e")[one, :], ALU.subtract))
            link(eng.tensor_scalar(c_int[one, :], c_cnt[one, :], float(P - 1), None, ALU.add))
            link(eng.tensor_scalar(c_sh[one, :], c_int[one, :], 7, None, ALU.logical_shift_right))
            link(eng.tensor_copy(n_t[one, :], c_sh[one, :]))
            link(eng.tensor_copy(cum[one, 0:1], n_t[one, 0:1]))
            for n in range(1, n_exp):
                link(eng.tensor_tensor(cum[one, n:n + 1], cum[one, n - 1:n], n_t[one, n:n + 1], ALU.add))
            eng.memset(t_exp[one, :], 0.0)
            link(eng.memset(t_prev[one, :], 0.0))
            no = const("tile_no")[one, :]
            for n in range(n_exp - 1):
                link(eng.tensor_scalar(t_ge[one, :], no, cum[one, n:n + 1], None, ALU.is_ge))
                link(eng.tensor_tensor(t_exp[one, :], t_exp[one, :], t_ge[one, :], ALU.add))
                link(eng.scalar_tensor_tensor(out=t_prev[one, :], in0=t_ge[one, :], scalar=n_t[one, n:n + 1],
                                              in1=t_prev[one, :], op0=ALU.mult, op1=ALU.add))
            link(eng.tensor_tensor(t_prev[one, :], no, t_prev[one, :], ALU.subtract))
            link(eng.tensor_scalar(t_base[one, :], t_exp[one, :], float(region), None, ALU.mult))
            link(eng.scalar_tensor_tensor(out=t_base[one, :], in0=t_prev[one, :], scalar=float(P), in1=t_base[one, :],
                                          op0=ALU.mult, op1=ALU.add))
            link(eng.tensor_scalar(t_ge[one, :], no, cum[one, n_exp - 1:n_exp], None, ALU.is_ge))
            link(eng.tensor_scalar(t_dif[one, :], t_base[one, :], -1.0, float(n_exp * region), ALU.mult, ALU.add))
            link(eng.tensor_tensor(t_dif[one, :], t_dif[one, :], t_ge[one, :], ALU.mult))
            link(eng.tensor_tensor(t_base[one, :], t_base[one, :], t_dif[one, :], ALU.add))
            link(eng.tensor_copy(tile_base[one, :], t_base[one, :]))
            eng.tensor_copy(tile_exp[one, :], t_exp[one, :]).then_inc(table_ready, 1)

            U = [KV[:, 0:512], KV[:, 512:1024]]

            def tile_step(at):
                if t := at(2):
                    wait(t, down_done)
                    wait_ring(t, added, RING)
                    s = t.slot(RING)
                    eng.tensor_scalar(yw[:, s, :], YY[:, 0:P], xg[:, s, P:P + 1], None, ALU.mult).then_inc(yw_ready, 1)
                    eng.tensor_copy(tok_i[:, s, :], xg[:, s, P + 1:ROW]).then_inc(tok_ready, 1)
                if t := at(1):
                    wait(t, sil_ready)
                    wait(t, ht_done, 2)
                    eng.tensor_tensor(hid[:, t.slot(2), :], U[t.slot(2)], sil[:, t.slot(2), :], ALU.mult).then_inc(hid_ready, 1)

            run_steps(eng, n_tiles, B_FIRST, B_LAGS, tile_step)

            def last_norm(at):
                if c := at(0):
                    s = c.slot(2)
                    wait_ring(c, fin_in)
                    wait(c, fmv_ready, 2)
                    for n in range(C_SLICES):
                        ins = eng.bn_stats(fstat[:, s, n, :], fin[:, c.slot(RING), n, :])
                    ins.then_inc(fstat_ready, 1)
                    wait(c, fstat_ready)
                    wait(c, fout_ready, 2)
                    stand(c, 3)
                    for n in range(C_SLICES):
                        ins = eng.bn_aggr(fmv[:, s, n, :], fstat[:, s, n, :])
                    ins.then_inc(fmv_ready, 1)
                if c := at(1):
                    s = c.slot(2)
                    wait(c, frs_ready)
                    for n in range(C_SLICES):
                        ins = eng.tensor_scalar(fin[:, c.slot(RING), n, :], fin[:, c.slot(RING), n, :],
                                                fmv[:, s, n, 0:1], frs[:, s, n:n + 1], ALU.subtract, ALU.mult)
                    ins.then_inc(fout_ready, 1)

            run_steps(eng, n_chunks_c, C_FIRST, C_LAGS, last_norm)

        @block.gpsimd
        def _(eng):
            eng.memset(eps_c[:, :], EPS)
            eng.memset(half_c[:, :], -0.5).then_inc(pool_consts, 1)
            eng.wait_ge(pool_consts, 1)
            eng.wait_ge(tab_in, 16)

            def rstd(it, mv, ve, rs, mv_ready, ve_ready, rs_ready, used):
                s = it.slot(2)
                wait(it, mv_ready)
                wait(it, rs_ready, 2)
                eng.tensor_tensor(ve[:, s, :], mv[:, s, :, 1], eps_c[:, 0:2], ALU.add).then_inc(ve_ready, 1)
                wait(it, ve_ready)
                wait(it, used, 2)
                eng.tensor_tensor(rs[:, s, :], ve[:, s, :], half_c[:, 0:2], ALU.pow).then_inc(rs_ready, 1)

            def step(at):
                a, b, c, d, e = (at(lag) for lag in (1, 2, 3, 4, 5))
                if c:
                    rstd(c, mv1, ve1, rs1, mv1_ready, ve1_ready, rs1_ready, x1_ready)
                if d:
                    rstd(d, mv2, ve2, rs2, mv2_ready, ve2_ready, rs2_ready, x2_ready)
                if b:
                    wait_ring(b, ctx_in)
                    cs = ctx_sb[:, b.slot(RING), :, :]
                    wait(b, xk_ready, 1)
                    eng.tensor_tensor(xk_a[:, :, :], cs, twice(const("ck")), ALU.mult).then_inc(xka_ready, 1)
                    for u in range(2):
                        ins = eng.tensor_tensor(couples(xk_b[:, u, :]), swapped(cs[:, u, :]), couples(const("sk")), ALU.mult)
                    ins.then_inc(xkb_ready, 1)
                    wait(b, xka_ready)
                    wait(b, xkb_ready)
                    wait(b, kv_ready, 1)
                    eng.tensor_tensor(xk[:, :, :], xk_a[:, :, :], xk_b[:, :, :], ALU.add).then_inc(xk_ready, 1)
                    wait(b, xk_ready)
                    wait(b, kv_done[3], 2)
                    for u in range(2):
                        ins = eng.tensor_tensor(
                            kv[:, b.slot(2), u, :].rearrange("p (h j i) -> p h j i", j=HD, i=HD),
                            xk[:, u, :].rearrange("p (h i) -> p h i", i=HD).unsqueeze(2).to_broadcast([P, NH, HD, HD]),
                            cs[:, u, :].rearrange("p (h j) -> p h j", j=HD).unsqueeze(3).to_broadcast([P, NH, HD, HD]),
                            ALU.mult)
                    ins.then_inc(kv_ready, 1)
                if e:
                    r = e.slot(RING)
                    wait(e, w2_ready)
                    eng.tensor_copy(xe[:, r, :, :, P + 1],
                                    const("ids")[:, bass.ds(e.number() * 2, 2)].unsqueeze(2).to_broadcast([P, 2, 2])
                                    ).then_inc(id_ready, 1)
                    wait(e, pos_ready)
                    wait(e, id_ready)
                    stand(e, 4)
                    for n in range(4):
                        eng.indirect_dma_start(out=xs, out_offset=bass.IndirectOffsetOnAxis(ap=pos[:, r, n:n + 1], axis=0),
                                               in_=xe[:, r, n // 2, n % 2, :], in_offset=None).then_inc(routed_out[r], 16)
                if a:
                    s = a.slot(2)
                    wait(a, e_ready)
                    wait(a, oraw_ready, 1)
                    for u in range(2):
                        ins = eng.tensor_tensor(
                            prod_ev[:, u, :, :, :],
                            e_sb[:, s, u, :].rearrange("p (i j) -> p i j", j=NH).unsqueeze(2).to_broadcast([P, NH, HD, NH]),
                            qkv[:, s, u, 2 * P:3 * P].rearrange("p (d j) -> p d j", j=NH).unsqueeze(1).to_broadcast([P, NH, HD, NH]),
                            ALU.mult)
                    ins.then_inc(ev_ready, 1)

            run_steps(eng, n_duo, A_FIRST, A_LAGS, step)

            eng.wait_ge(padi_ready, 1)
            for n in range(n_exp):
                eng.indirect_dma_start(out=xs, out_offset=bass.IndirectOffsetOnAxis(ap=pad_i[:, n:n + 1], axis=0),
                                       in_=pad_rows[:, :], in_offset=None).then_inc(pads_out, 16)
            eng.dma_start(xs[n_exp * region:n_exp * region + P, :], pad_rows[:, :]).then_inc(pads_out, 16)
            for r in range(RING):
                eng.wait_ge(acc_out[r], 16 * n_duo // RING)
            eng.wait_ge(spare_out, 16)

            def add_tile(at):
                if t := at(3):
                    s = t.slot(RING)
                    wait(t, yw_ready)
                    wait(t, tok_ready)
                    wait_ring(t, added, 1)
                    stand(t, 5)
                    eng.indirect_dma_start(out=acc, out_offset=bass.IndirectOffsetOnAxis(ap=tok_i[:, s, :], axis=0),
                                           in_=yw[:, s, :], in_offset=None, compute_op=ALU.add).then_inc(added[s], 16)

            run_steps(eng, n_tiles, B_FIRST, B_LAGS, add_tile)

            def last_norm(at):
                if c := at(0):
                    s = c.slot(2)
                    wait(c, fmv_ready)
                    wait(c, frs_ready, 2)
                    eng.tensor_tensor(fve[:, s, :], fmv[:, s, :, 1], eps_c[:, 0:C_SLICES], ALU.add).then_inc(fve_ready, 1)
                    wait(c, fve_ready)
                    wait(c, fout_ready, 2)
                    eng.tensor_tensor(frs[:, s, :], fve[:, s, :], half_c[:, 0:C_SLICES], ALU.pow).then_inc(frs_ready, 1)

            run_steps(eng, n_chunks_c, C_FIRST, C_LAGS, last_norm)


def kernel(x, ctx_1024, L0_attn_Wq, L0_attn_Wk, L0_attn_Wv, L0_attn_Wo, L0_attn_bo, L0_ffn_gate,
           L0_ffn_experts_w1, L0_ffn_experts_w2, L0_ffn_experts_w3):
    import concourse.bacc as bacc
    from concourse.bass_utils import run_bass_kernel_spmd

    shape = x.shape
    n_tok = shape[0] * shape[1]
    n_exp = L0_ffn_experts_w1.shape[0]
    table, where = constants(n_tok, n_exp)
    by_dim = np.arange(P).reshape(NH, HD).T.ravel()
    w_qkv = [np.asarray(w).T[:, by_dim] for w in (L0_attn_Wq, L0_attn_Wk, L0_attn_Wv)]
    wo = np.asarray(L0_attn_Wo).T.reshape(NH, HD, P)
    arrays = {
        "x": np.asarray(x).reshape(n_tok, P),
        "ctx": np.asarray(ctx_1024).reshape(n_tok, P),
        "w_qkv": np.concatenate(w_qkv, 1),
        "wo_by_token": np.ascontiguousarray(wo[np.arange(P) % NH]),
        "bo": np.asarray(L0_attn_bo).reshape(P, 1),
        "gate": np.asarray(L0_ffn_gate),
        "w1": np.asarray(L0_ffn_experts_w1),
        "w3": np.asarray(L0_ffn_experts_w3),
        "w2": np.asarray(L0_ffn_experts_w2),
        "table": table,
    }
    nc = bacc.Bacc("TRN2", target_bir_lowering=False, num_devices=1)
    aps = {n: nc.dram_tensor(n, a.shape, mybir.dt.from_np(a.dtype), kind="ExternalInput").ap() for n, a in arrays.items()}
    out = nc.dram_tensor("out", (n_tok, P), F32, kind="ExternalOutput").ap()
    build(nc, **aps, where=where, out=out)
    result = run_bass_kernel_spmd(nc, [arrays], core_ids=[0])
    return result.results[0]["out"].reshape(shape)
```

```python
from contextlib import ExitStack

import numpy as np

import concourse.bass as bass
from concourse import mybir
from concourse.alu_op_type import AluOpType as ALU

ACT = mybir.ActivationFunctionType
AX = mybir.AxisListType
F32 = mybir.dt.float32
BF16 = mybir.dt.bfloat16
I32 = mybir.dt.int32
U32 = mybir.dt.uint32

P = 128
S = 64
NH = 16
HD = 8
UNROLL = 4
RING = 4
ROW = P + 2
EPS = 1e-5


def constants(n_tok, n_exp):
    p = np.arange(P)
    b, t = p // S, p % S
    d = np.arange(P)
    head, r = d // HD, d % HD
    e = r // 2
    gam = 1.0 - np.exp(np.linspace(np.log(1.0 / 32.0), np.log(1.0 / 512.0), P // HD))
    base = (2.0 * np.arange(HD // 2) + 0.4 * HD) / (1.4 * HD)
    inv = 1.0 / 10000.0 ** (np.arange(HD // 2) / (HD // 2))
    ang = t[:, None] * inv[e][None, :]
    scale = base[e][None, :] ** (t[:, None] / 512.0)
    decay = gam[head][None, :] ** t[:, None]
    sign = np.where(r % 2 == 0, -1.0, 1.0)[None, :]
    same = b[:, None] == b[None, :]
    parts = {
        "ident": np.eye(P),
        "tri": same & (t[:, None] <= t[None, :]),
        "before": p[:, None] < p[None, :],
        "group": p[:, None] // NH == np.arange(P // NH),
        "cq": np.cos(ang) * scale * decay,
        "sq": np.sin(ang) * scale * decay * sign,
        "ck": np.cos(ang) / scale / decay,
        "sk": np.sin(ang) / scale / decay * sign,
        "iota_e": np.broadcast_to(np.arange(n_exp), (P, n_exp)),
        "base_e": np.broadcast_to(np.arange(n_exp) * (n_tok + P), (P, n_exp)),
        "lane": p[:, None],
        "spare_ids": 2 * n_tok + p[:, None] + P * np.arange(2 * n_exp)[None, :],
        "ids": 2 * p[:, None] + 2 * P * (np.arange(2 * n_tok // P) // 2) + np.arange(2 * n_tok // P) % 2,
        "tile_no": np.broadcast_to(np.arange(2 * n_tok // P + n_exp), (P, 2 * n_tok // P + n_exp)),
    }
    where, at = {}, 0
    for name, a in parts.items():
        n = int(np.prod(a.shape[1:]))
        where[name] = (at, at + n)
        at += n
    table = np.concatenate([np.asarray(a, np.float64).reshape(P, -1) for a in parts.values()], 1)
    return table.astype(np.float32), where


class Item:

    def __init__(self, eng, i, snaps, off):
        self.eng, self.i, self.snaps, self.off = eng, i, snaps, off

    def slot(self, n):
        return self.off % n

    def number(self, lo=0, hi=None):
        return self.off if self.i is None else self.i * UNROLL + self.off

    def count(self, back=0):
        n = self.off + 1 - back
        if self.i is None:
            return n
        assert n > 0
        key = (UNROLL, n)
        if key not in self.snaps:
            self.snaps[key] = self.eng.snap(self.i * UNROLL + n)
        return self.snaps[key]

    def ring_count(self, per, back=0):
        n = (self.off - back) // RING + 1
        if self.i is None:
            return per * n
        assert n > 0
        key = (per, n)
        if key not in self.snaps:
            self.snaps[key] = self.eng.snap((self.i + n) * per)
        return self.snaps[key]


def wait(item, sem, back=0):
    if item.i is None and item.off + 1 - back <= 0:
        return
    item.eng.wait_ge(sem, item.count(back))


def wait_ring(item, sems, back=0, per=16):
    if item.i is None and item.off - back < 0:
        return
    item.eng.wait_ge(sems[(item.off - back) % RING], item.ring_count(per, back))


def run_steps(eng, n, first, lags, body):
    def alone(s):
        body(lambda lag: Item(eng, None, None, s - lag) if 0 <= s - lag < n else None)

    for s in range(first):
        alone(s)
    if n > first:
        with eng.Fori(0, (n - first) // UNROLL) as i:
            snaps = {}
            for k in range(UNROLL):
                body(lambda lag, k=k: Item(eng, i, snaps, first + k - lag))
    for s in range(n, n + lags):
        alone(s)


def build(nc, x, ctx, w_qkv, wo_by_token, bo, gate, w1, w3, w2, table, where, out):
    n_tok = x.shape[0]
    n_exp, inner = w1.shape[0], w1.shape[2]
    n_chunk = inner // P
    n_duo = n_tok // (2 * P)
    region = n_tok + P
    n_tiles = 2 * n_tok // P + n_exp
    A_FIRST, A_LAGS = 12, 8
    B_FIRST, B_LAGS = 8, 3
    C_SLICES = 4
    n_chunks_c = n_tok // P // C_SLICES
    C_FIRST, C_LAGS = 4, 2
    assert (n_duo - A_FIRST) % UNROLL == 0 and (n_tiles - B_FIRST) % UNROLL == 0

    xs = nc.dram_tensor("routed_rows", [n_exp * (region + P), ROW], F32).ap()
    halves = nc.dram_tensor("token_halves", [2 * n_tok + 2 * n_exp * P, P], F32).ap()

    x_duos = x.rearrange("(n u p) d -> n p u d", u=2, p=P)
    ctx_duos = ctx.rearrange("(n u p) d -> n p u d", u=2, p=P)
    half_rows = halves[0:2 * n_tok, :].rearrange("(p n k) d -> p n k d", p=P, k=2)
    out_rows = out.rearrange("(p n) d -> p n d", p=P)

    with ExitStack() as stack:
        def sb(name, shape, dt=F32):
            return stack.enter_context(nc.sbuf_tensor(name, [P, *shape], dt))

        def ps(name, n):
            return stack.enter_context(nc.psum_tensor(name, [P, n], F32))

        def sem(name):
            return stack.enter_context(nc.semaphore(name))

        def ring_sem(name):
            return [sem(f"{name}{i}") for i in range(RING)]

        tab = sb("tab", [table.shape[1]])

        def const(name):
            a, b = where[name]
            return tab[:, a:b]

        ident, tri = const("ident"), const("tri")
        w_qkv_sb = sb("w_qkv_sb", [3 * P])
        wo_sb = sb("wo_sb", [HD, P])
        bo_sb = sb("bo_sb", [1])
        gate_sb = sb("gate_sb", [n_exp])
        w1_sb = sb("w1_sb", [n_exp * inner])
        w3_sb = sb("w3_sb", [n_exp * inner])
        w2_sb = sb("w2_sb", [n_exp * inner])
        before_bf = sb("before_bf", [P], BF16)
        ones_bf = sb("ones_bf", [P], BF16)
        eps_c = sb("eps_c", [8])
        half_c = sb("half_c", [8])

        x_sb, x_res, ctx_sb = (sb(n, [RING, 2, P]) for n in ("x_sb", "x_res", "ctx_sb"))
        x_t = sb("x_t", [2, 2, P])
        qkv = sb("qkv", [RING, 2, 3 * P])
        prod_qk = sb("prod_qk", [2, HD, NH * NH])
        m_sb = sb("m_sb", [2, NH])
        s_m = sb("s_m", [2, NH * NH])
        e_sb = sb("e_sb", [2, 2, NH * NH])
        den, r_den = sb("den", [2, NH]), sb("r_den", [2, 2, NH])
        prod_ev = sb("prod_ev", [2, NH, HD, NH])
        o_raw = sb("o_raw", [2, P])
        o_n = sb("o_n", [2, 2, HD, NH])
        o_g = sb("o_g", [2, HD, HD, NH])
        y_t = sb("y_t", [2, P])
        res1, res2 = sb("res1", [2, 2, P]), sb("res2", [2, 2, P])
        stat1, stat2 = sb("stat1", [2, 2, 6]), sb("stat2", [2, 2, 6])
        mv1, mv2 = sb("mv1", [2, 2, 2]), sb("mv2", [2, 2, 2])
        ve1, ve2 = sb("ve1", [2, 2]), sb("ve2", [2, 2])
        rs1, rs2 = sb("rs1", [2, 2]), sb("rs2", [2, 2])
        nb1, nb2 = sb("nb1", [2, 2]), sb("nb2", [2, 2])
        x1 = sb("x1", [2, 2, P])
        xq_a, xq_b, xq = sb("xq_a", [2, P]), sb("xq_b", [2, P]), sb("xq", [2, P])
        xk_a, xk_b, xk = sb("xk_a", [2, P]), sb("xk_b", [2, P]), sb("xk", [2, P])
        kv = sb("kv", [2, 2, 1024])
        prod_kv = sb("prod_kv", [2, 1024])
        ret = sb("ret", [2, P])
        xe = sb("xe", [RING, 2, 2, ROW])
        x2_t = sb("x2_t", [2, 2, P])
        lg = sb("lg", [2, 2, n_exp])
        mx8, ix8 = sb("mx8", [2, 2, 8]), sb("ix8", [2, 2, 8], U32)
        dlt, ex, dn = sb("dlt", [2, 2]), sb("ex", [2, 2]), sb("dn", [2, 2])
        oh = sb("oh", [2, 2, 2, n_exp])
        ohs = sb("ohs", [2, 2, n_exp], BF16)
        cnt = sb("cnt", [n_exp])
        posf, posw = sb("posf", [2, n_exp]), sb("posw", [2, 2, n_exp])
        pos = sb("pos", [RING, 4], I32)

        pad_f, pad_i = sb("pad_f", [n_exp]), sb("pad_i", [n_exp], I32)
        c_cnt, c_int, c_sh = sb("c_cnt", [n_exp]), sb("c_int", [n_exp], I32), sb("c_sh", [n_exp], I32)
        n_t, cum = sb("n_t", [n_exp]), sb("cum", [n_exp])
        t_ge, t_exp, t_prev, t_base, t_dif = (sb(n, [n_tiles]) for n in ("t_ge", "t_exp", "t_prev", "t_base", "t_dif"))
        tile_exp, tile_base = sb("tile_exp", [n_tiles], I32), sb("tile_base", [n_tiles], I32)

        pads = prod_ev[:, :, :, :, :].rearrange("p u i d j -> p (u i d j)")[:, 0:2 * n_exp * ROW].rearrange(
            "p (n c) -> p n c", c=ROW)

        xg = sb("xg", [RING, ROW])
        xg_t = sb("xg_t", [2, P])
        stage_b = prod_qk[:, :, :, :].rearrange("p u d i -> p (u d i)")
        sil, hid, hid_t = (stage_b[:, n * 2 * inner:(n + 1) * 2 * inner].rearrange("p (s i) -> p s i", s=2)
                           for n in range(3))
        xh = sb("xh", [2, P])
        yw = sb("yw", [RING, P])
        tok_i = sb("tok_i", [RING, 1], I32)

        fin = prod_ev[:, :, :, :, :].rearrange("p u i d j -> p (u i d j)").rearrange(
            "p (r n k d) -> p r n k d", r=RING, n=C_SLICES, k=2)
        fstat, fmv = sb("fstat", [2, C_SLICES, 6]), sb("fmv", [2, C_SLICES, 2])
        fve, frs = sb("fve", [2, C_SLICES]), sb("frs", [2, C_SLICES])

        XT, SC, YY, TR = ps("XT", 512), ps("SC", 512), ps("YY", 512), ps("TR", 512)
        QKV, KV = ps("QKV", 1024), ps("KV", 1024)
        qkv_ps = QKV[:, :].rearrange("p (u c) -> p u c", u=2)[:, :, 0:3 * P]
        YT, Y = YY[:, 0:2 * P], YY[:, 2 * P:4 * P]
        X2T, LG, RANK = TR[:, 0:2 * P], TR[:, 256:256 + 2 * n_exp], XT[:, 256:256 + 3 * n_exp]

        tab_in, small_in, big_in = sem("tab_in"), sem("small_in"), sem("big_in")
        consts_ready, pool_consts = sem("consts_ready"), sem("pool_consts")
        xt_done, qkv_done, x2t_done, logit_done, yt_done, y_done, rank_done = (
            sem(n) for n in ("xt_done", "qkv_done", "x2t_done", "logit_done", "yt_done", "y_done",
                             "rank_done"))
        score_done = [sem(f"score_done{u}") for u in range(2)]
        oraw_ready = [sem(f"oraw_ready{u}") for u in range(2)]
        kv_done = [sem(f"kv_done{n}") for n in range(4)]
        xt_ready, qkv_ready, e_ready, og_ready, yt_ready, x2t_ready, ex_ready = (
            sem(n) for n in ("xt_ready", "qkv_ready", "e_ready", "og_ready", "yt_ready", "x2t_ready", "ex_ready"))
        qk_ready = [sem(f"qk_ready{u}") for u in range(2)]
        kvp_ready = [sem(f"kvp_ready{n}") for n in range(4)]
        m_ready, sm_ready, den_ready, rden_ready, on_ready = (
            sem(n) for n in ("m_ready", "sm_ready", "den_ready", "rden_ready", "on_ready"))
        lg_ready, mx_ready, ix_ready, oh_ready, ohs_ready, dlt_ready = (
            sem(n) for n in ("lg_ready", "mx_ready", "ix_ready", "oh_ready", "ohs_ready", "dlt_ready"))
        res2_ready, stat2_ready, mv2_ready, res1_ready, stat1_ready, mv1_ready, ret_ready = (
            sem(n) for n in ("res2_ready", "stat2_ready", "mv2_ready", "res1_ready", "stat1_ready", "mv1_ready",
                             "ret_ready"))
        nb1_ready, nb2_ready, x1_ready, x2_ready, dn_ready, w1_ready, w2_ready = (
            sem(n) for n in ("nb1_ready", "nb2_ready", "x1_ready", "x2_ready", "dn_ready", "w1_ready", "w2_ready"))
        xqa_ready, xqb_ready, xq_ready = (sem(n) for n in ("xqa_ready", "xqb_ready", "xq_ready"))
        posf_ready, cnt_ready, posw_ready, pos_ready = (
            sem(n) for n in ("posf_ready", "cnt_ready", "posw_ready", "pos_ready"))
        xka_ready, xkb_ready, xk_ready, kv_ready, id_ready = (
            sem(n) for n in ("xka_ready", "xkb_ready", "xk_ready", "kv_ready", "id_ready"))
        ev_ready = [sem(f"ev_ready{u}") for u in range(2)]
        ve1_ready, rs1_ready, ve2_ready, rs2_ready = (
            sem(n) for n in ("ve1_ready", "rs1_ready", "ve2_ready", "rs2_ready"))
        x_in, x_res_in, ctx_in, routed_out = (ring_sem(n) for n in ("x_in", "x_res_in", "ctx_in", "routed_out"))
        chain, padi_ready, table_ready, pads_out = sem("chain"), sem("padi_ready"), sem("table_ready"), sem("pads_out")
        xg_in, half_out = ring_sem("xg_in"), ring_sem("half_out")
        xgt_done, g_done, u_done, ht_done, down_done = (
            sem(n) for n in ("xgt_done", "g_done", "u_done", "ht_done", "down_done"))
        xgt_ready, sil_ready, ht_ready, xh_ready = (sem(n) for n in ("xgt_ready", "sil_ready", "ht_ready", "xh_ready"))
        hid_ready, yw_ready, tok_ready = (sem(n) for n in ("hid_ready", "yw_ready", "tok_ready"))
        fin_in, fin_out = ring_sem("fin_in"), ring_sem("fin_out")
        fsum_ready, fstat_ready, fmv_ready, fve_ready, frs_ready, fout_ready = (
            sem(n) for n in ("fsum_ready", "fstat_ready", "fmv_ready", "fve_ready", "frs_ready", "fout_ready"))

        marks = sb("marks", [6])
        marked = [sem(f"marked{n}") for n in range(6)]

        def stand(it, n):
            wait(it, marked[n], 1)
            if n < 4:
                it.eng.memset(marks[:, n:n + 1], 0.0).then_inc(marked[n], 1)
            else:
                it.eng.tensor_tensor(marks[:, n:n + 1], half_c[:, 0:1], half_c[:, 0:1], ALU.add).then_inc(marked[n], 1)

        def swapped(ap):
            return couples(ap)[:, :, ::-1]

        def couples(ap):
            return ap.rearrange("p (e w) -> p e w", w=2)

        def twice(ap):
            return ap.unsqueeze(1).to_broadcast([P, 2, ap.shape[1]])

        block = stack.enter_context(nc.Block())

        @block.sync
        def _(eng):
            eng.dma_start(tab[:, :], table).then_inc(tab_in, 16)
            eng.dma_start(w_qkv_sb[:, :], w_qkv).then_inc(small_in, 16)
            eng.dma_start(wo_sb[:, :, :], wo_by_token).then_inc(small_in, 16)
            eng.dma_start(bo_sb[:, :], bo).then_inc(small_in, 16)
            eng.dma_start(gate_sb[:, :], gate).then_inc(small_in, 16)
            def step(at):
                if it := at(0):
                    wait(it, xt_done, RING)
                    eng.dma_start(x_sb[:, it.slot(RING), :, :], x_duos[it.number()]).then_inc(x_in[it.slot(RING)], 16)
                if it := at(3):
                    wait(it, res1_ready, RING)
                    eng.dma_start(x_res[:, it.slot(RING), :, :], x_duos[it.number()]).then_inc(x_res_in[it.slot(RING)], 16)
                    wait(it, kv_ready, RING)
                    eng.dma_start(ctx_sb[:, it.slot(RING), :, :], ctx_duos[it.number()]).then_inc(ctx_in[it.slot(RING)], 16)

            run_steps(eng, n_duo, A_FIRST, A_LAGS, step)

            for r in range(RING):
                eng.wait_ge(routed_out[r], 64 * n_duo // RING)
            eng.wait_ge(pads_out, 16 * (n_exp + 1))
            eng.wait_ge(table_ready, 1)

            def load_tile(at):
                if t := at(0):
                    row = eng.value_load(tile_base[0:1, bass.ds(t.number(), 1)], min_val=0, max_val=(n_exp - 1) * P + n_exp * region)
                    wait(t, yw_ready, RING)
                    wait(t, tok_ready, RING)
                    wait(t, xh_ready, RING)
                    eng.dma_start(xg[:, t.slot(RING), :], xs[bass.ds(row, P), :]).then_inc(xg_in[t.slot(RING)], 16)

            run_steps(eng, n_tiles, B_FIRST, 0, load_tile)

            for r in range(RING):
                eng.wait_ge(half_out[r], 16 * n_tiles // RING)

            def last_norm(at):
                if c := at(0):
                    wait_ring(c, fin_out, RING)
                    eng.dma_start(fin[:, c.slot(RING), :, :, :],
                                  half_rows[:, bass.ds(c.number() * C_SLICES, C_SLICES), :, :]).then_inc(fin_in[c.slot(RING)], 16)
                if c := at(2):
                    wait(c, fout_ready)
                    eng.dma_start(out_rows[:, bass.ds(c.number() * C_SLICES, C_SLICES), :],
                                  fin[:, c.slot(RING), :, 0, :]).then_inc(fin_out[c.slot(RING)], 16)

            run_steps(eng, n_chunks_c, C_FIRST, C_LAGS, last_norm)
            for r in range(RING):
                eng.wait_ge(fin_out[r], 16 * n_chunks_c // RING)

        @block.tensor
        def _(eng):
            eng.wait_ge(tab_in, 16)
            eng.wait_ge(small_in, 16 * 4)
            eng.wait_ge(consts_ready, 1)

            def step(at):
                z, a, m, y, c, d, e = (at(lag) for lag in (1, 2, 3, 5, 6, 7, 8))

                def kv_sums(n):
                    if n < 2:
                        wait(c, kvp_ready[n + 2], 1)
                    else:
                        wait(c, kvp_ready[n - 2])
                    eng.matmul(KV[:, 512 * (n % 2):512 * (n % 2) + 512], tri,
                               kv[:, c.slot(2), n // 2, 512 * (n % 2):512 * (n % 2) + 512],
                               start=True, stop=True).then_inc(kv_done[n], 1)

                def scores(it, u):
                    wait(it, qk_ready[u])
                    wait(it, sm_ready, 1)
                    for n in range(HD):
                        mm = eng.matmul(SC[:, 256 * u:256 * u + 256], ident, prod_qk[:, u, n, :],
                                        start=(n == 0), stop=(n == HD - 1))
                    mm.then_inc(score_done[u], 1)

                if m:
                    scores(m, 1)
                if c:
                    wait(c, kv_ready)
                    kv_sums(0)
                    kv_sums(1)
                if z:
                    wait_ring(z, x_in)
                    wait(z, xt_ready, 1)
                    wait(z, posf_ready, 8)
                    wait(z, cnt_ready, 8)
                    for u in range(2):
                        mm = eng.transpose(XT[:, P * u:P * u + P], x_sb[:, z.slot(RING), u, :], ident)
                    mm.then_inc(xt_done, 1)
                if y:
                    wait(y, og_ready)
                    wait(y, res1_ready, 1)
                    for n in range(HD):
                        mm = eng.matmul(YT, wo_sb[:, n, :], o_g[:, :, n, :, :].rearrange("p u g h -> p u (g h)"),
                                        start=(n == 0), stop=(n == HD - 1))
                    mm.then_inc(yt_done, 1)
                if d:
                    wait(d, x2_ready)
                    wait(d, lg_ready, 1)
                    for u in range(2):
                        mm = eng.transpose(X2T[:, P * u:P * u + P], xe[:, d.slot(RING), u, 0, 0:P], ident)
                    mm.then_inc(x2t_done, 1)
                if z:
                    wait(z, xt_ready)
                    wait(z, qkv_ready, 1)
                    for u in range(2):
                        mm = eng.matmul(qkv_ps[:, u, :], x_t[:, z.slot(2), u, :], w_qkv_sb[:, :], start=True, stop=True)
                    mm.then_inc(qkv_done, 1)
                if d:
                    wait(d, x2t_ready)
                    for u in range(2):
                        mm = eng.matmul(LG[:, n_exp * u:n_exp * u + n_exp], x2_t[:, d.slot(2), u, :], gate_sb[:, :],
                                        start=True, stop=True)
                    mm.then_inc(logit_done, 1)
                if c:
                    kv_sums(2)
                    kv_sums(3)
                if y:
                    wait(y, yt_ready)
                    for u in range(2):
                        mm = eng.transpose(Y[:, P * u:P * u + P], y_t[:, u, :], ident)
                    mm.then_inc(y_done, 1)
                if e:
                    wait(e, ohs_ready)
                    o = ohs[:, e.slot(2), :, :]
                    eng.matmul(RANK[:, 0:2 * n_exp], before_bf[:, :], o.rearrange("p u e -> p (u e)"),
                               start=True, stop=False, skip_group_check=True)
                    eng.matmul(RANK[:, n_exp:2 * n_exp], ones_bf[:, :], o[:, 0, :], start=False, stop=True,
                               skip_group_check=True)
                    for u in range(2):
                        mm = eng.matmul(RANK[:, 2 * n_exp:3 * n_exp], ones_bf[:, :], o[:, u, :],
                                        start=(u == 0), stop=(u == 1), skip_group_check=True)
                    mm.then_inc(rank_done, 1)
                if a:
                    scores(a, 0)

            run_steps(eng, n_duo, A_FIRST, A_LAGS, step)

            eng.wait_ge(big_in, 16 * (2 + n_chunk))
            eng.wait_ge(table_ready, 1)
            eng.wait_ge(pos_ready, n_duo)
            G = [QKV[:, 0:512], QKV[:, 512:1024]]
            U = [KV[:, 0:512], KV[:, 512:1024]]
            HT = [XT, SC]

            def tile_step(at):
                t, up, down = at(0), at(1), at(2)
                if up:
                    up_no = eng.value_load(tile_exp[0:1, bass.ds(up.number(), 1)], min_val=0, max_val=n_exp - 1)
                    cols = bass.ds(up_no * inner, inner)
                if down:
                    down_no = eng.value_load(tile_exp[0:1, bass.ds(down.number(), 1)], min_val=0, max_val=n_exp - 1)
                    wait(down, hid_ready)
                    wait(down, ht_ready, 2)
                    for n in range(n_chunk):
                        mm = eng.transpose(HT[down.slot(2)][:, P * n:P * n + P], hid[:, down.slot(2), P * n:P * n + P], ident)
                    mm.then_inc(ht_done, 1)
                if up:
                    wait(up, xgt_ready)
                    wait(up, sil_ready, 2)
                    eng.matmul(G[up.slot(2)], xg_t[:, up.slot(2), :], w1_sb[:, cols], start=True, stop=True).then_inc(g_done, 1)
                    wait(up, hid_ready, 2)
                    eng.matmul(U[up.slot(2)], xg_t[:, up.slot(2), :], w3_sb[:, cols], start=True, stop=True).then_inc(u_done, 1)
                if t:
                    wait_ring(t, xg_in)
                    wait(t, xgt_ready, 1)
                    eng.transpose(TR[:, 0:P], xg[:, t.slot(RING), 0:P], ident).then_inc(xgt_done, 1)
                if down:
                    wait(down, ht_ready)
                    wait(down, yw_ready, 1)
                    for n in range(n_chunk):
                        mm = eng.matmul(YY[:, 0:P], hid_t[:, down.slot(2), P * n:P * n + P],
                                        w2_sb[:, bass.ds(down_no * inner + P * n, P)],
                                        start=(n == 0), stop=(n == n_chunk - 1))
                    mm.then_inc(down_done, 1)

            run_steps(eng, n_tiles, B_FIRST, B_LAGS, tile_step)

        @block.scalar
        def _(eng):
            eng.dma_start(w1_sb[:, :].rearrange("p (e i) -> p e i", e=n_exp), w1.rearrange("e h i -> h e i")).then_inc(big_in, 16)
            eng.dma_start(w3_sb[:, :].rearrange("p (e i) -> p e i", e=n_exp), w3.rearrange("e h i -> h e i")).then_inc(big_in, 16)
            w2_v = w2.rearrange("e (n p) h -> n p e h", p=P)
            w2_s = w2_sb[:, :].rearrange("p (e n h) -> p e n h", e=n_exp, n=n_chunk)
            for n in range(n_chunk):
                eng.dma_start(w2_s[:, :, n, :], w2_v[n]).then_inc(big_in, 16)
            eng.wait_ge(tab_in, 16)
            eng.wait_ge(small_in, 16 * 4)

            def step(at):
                z, a, b, y, c, d = (at(lag) for lag in (1, 3, 4, 5, 6, 7))
                if z:
                    wait(z, xt_done)
                    wait(z, qkv_done, 2)
                    eng.copy(x_t[:, z.slot(2), :, :].rearrange("p u t -> p (u t)"), XT[:, 0:2 * P]).then_inc(xt_ready, 1)
                if d:
                    s, r = d.slot(2), d.slot(RING)
                    wait(d, nb2_ready)
                    wait_ring(d, routed_out, RING, 64)
                    for u in range(2):
                        for k in range(2):
                            ins = eng.activation(xe[:, r, u, k, 0:P], res2[:, s, u, :], ACT.Identity,
                                                 bias=nb2[:, s, u:u + 1], scale=rs2[:, s, u:u + 1])
                    ins.then_inc(x2_ready, 1)
                if c:
                    s = c.slot(2)
                    wait(c, nb1_ready)
                    wait(c, res2_ready, 2)
                    wait(c, xqb_ready, 2)
                    for u in range(2):
                        ins = eng.activation(x1[:, s, u, :], res1[:, s, u, :], ACT.Identity,
                                             bias=nb1[:, s, u:u + 1], scale=rs1[:, s, u:u + 1])
                    ins.then_inc(x1_ready, 1)
                if a:
                    wait(a, sm_ready)
                    wait(a, ev_ready[1], 2)
                    wait(a, den_ready, 2)
                    eng.activation(e_sb[:, a.slot(2), :, :], s_m[:, :, :], ACT.Exp, scale=float(HD) ** -0.5).then_inc(e_ready, 1)
                if y:
                    wait(y, yt_done)
                    wait(y, y_done, 1)
                    for u in range(2):
                        ins = eng.activation(y_t[:, u, :].rearrange("p (b h g) -> p b g h", b=2, h=NH),
                                             YT[:, P * u:P * u + P].rearrange("p (b g h) -> p b g h", b=2, h=NH),
                                             ACT.Identity, bias=bo_sb[:, :])
                    ins.then_inc(yt_ready, 1)
                if d:
                    wait(d, x2t_done)
                    wait(d, logit_done, 2)
                    eng.copy(x2_t[:, d.slot(2), :, :].rearrange("p u t -> p (u t)"), X2T).then_inc(x2t_ready, 1)
                if z:
                    wait(z, qkv_done)
                    wait(z, ev_ready[1], RING)
                    wait(z, qk_ready[1], RING)
                    eng.copy(qkv[:, z.slot(RING), :, :], qkv_ps).then_inc(qkv_ready, 1)
                if b:
                    wait(b, on_ready)
                    wait(b, yt_done, 1)
                    for g in range(P // NH):
                        ins = eng.activation(o_g[:, :, :, g, :], o_n[:, b.slot(2), :, :, :], ACT.Copy,
                                             scale=const("group")[:, g:g + 1])
                    ins.then_inc(og_ready, 1)
                if d:
                    wait(d, dlt_ready)
                    wait(d, w2_ready, 2)
                    eng.activation(ex[:, d.slot(2), :], dlt[:, d.slot(2), :], ACT.Exp).then_inc(ex_ready, 1)

            run_steps(eng, n_duo, A_FIRST, A_LAGS, step)

            G = [QKV[:, 0:512], QKV[:, 512:1024]]
            HT = [XT, SC]

            def tile_step(at):
                if t := at(2):
                    wait(t, ht_done)
                    wait(t, down_done, 2)
                    eng.copy(hid_t[:, t.slot(2), :], HT[t.slot(2)][:, :]).then_inc(ht_ready, 1)
                if t := at(1):
                    wait_ring(t, xg_in)
                    wait(t, yw_ready, 2)
                    eng.mul(xh[:, t.slot(2), :], xg[:, t.slot(RING), 0:P], 0.5).then_inc(xh_ready, 1)
                    wait(t, g_done)
                    wait(t, hid_ready, 2)
                    eng.activation(sil[:, t.slot(2), :], G[t.slot(2)], ACT.Silu).then_inc(sil_ready, 1)
                if t := at(0):
                    wait(t, xgt_done)
                    wait(t, u_done, 2)
                    eng.copy(xg_t[:, t.slot(2), :], TR[:, 0:P]).then_inc(xgt_ready, 1)

            run_steps(eng, n_tiles, B_FIRST, B_LAGS, tile_step)

        @block.vector
        def _(eng):
            eng.memset(ones_bf[:, :], 1.0)
            eng.wait_ge(tab_in, 16)
            eng.tensor_copy(before_bf[:, :], const("before"))
            eng.tensor_copy(cnt[:, :], const("base_e")).then_inc(consts_ready, 1)
            eng.wait_ge(consts_ready, 1)

            def spread(it, res, stat, res_ready, stat_ready, mv_ready):
                wait(it, res_ready)
                wait(it, mv_ready, 2)
                for u in range(2):
                    ins = eng.bn_stats(stat[:, it.slot(2), u, :], res[:, it.slot(2), u, :])
                ins.then_inc(stat_ready, 1)

            def moments(it, mark, stat, mv, stat_ready, mv_ready, nb_ready):
                wait(it, stat_ready)
                wait(it, nb_ready, 2)
                stand(it, mark)
                for u in range(2):
                    ins = eng.bn_aggr(mv[:, it.slot(2), u, :], stat[:, it.slot(2), u, :])
                ins.then_inc(mv_ready, 1)

            def offset(it, mv, rs, nb, rs_ready, nb_ready, used):
                s = it.slot(2)
                wait(it, rs_ready)
                wait(it, used, 2)
                eng.scalar_tensor_tensor(out=nb[:, s, :], in0=mv[:, s, :, 0], scalar=-1.0, in1=rs[:, s, :],
                                         op0=ALU.mult, op1=ALU.mult).then_inc(nb_ready, 1)

            def step(at):
                a, m, b, y, c, d, e = (at(lag) for lag in (2, 3, 4, 5, 6, 7, 8))

                def times_sums(n):
                    u, h0 = n // 2, 8 * (n % 2)
                    wait(c, kv_done[n])
                    qv = xq[:, u, :].rearrange("p (h i) -> p h i", i=HD)[:, h0:h0 + 8, :]
                    eng.tensor_tensor(
                        prod_kv[:, u, 64 * h0:64 * h0 + 512].rearrange("p (h j i) -> p h j i", j=HD, i=HD),
                        KV[:, 512 * (n % 2):512 * (n % 2) + 512].rearrange("p (h j i) -> p h j i", j=HD, i=HD),
                        qv.unsqueeze(2).to_broadcast([P, 8, HD, HD]), ALU.mult).then_inc(kvp_ready[n], 1)

                if b:
                    wait(b, ev_ready[0])
                    wait(b, on_ready, 1)
                    eng.tensor_reduce(o_raw[:, 0, :], prod_ev[:, 0, :, :, :], AX.X, ALU.add).then_inc(oraw_ready[0], 1)
                if d:
                    offset(d, mv2, rs2, nb2, rs2_ready, nb2_ready, x2_ready)
                if m:
                    wait(m, score_done[0])
                    wait(m, score_done[1])
                    wait(m, sm_ready, 1)
                    sc = SC[:, :].rearrange("p (u i j) -> p (u i) j", u=2, j=NH)
                    eng.tensor_reduce(m_sb[:, :, :].rearrange("p u i -> p (u i)"), sc, AX.X, ALU.max).then_inc(m_ready, 1)
                if c:
                    offset(c, mv1, rs1, nb1, rs1_ready, nb1_ready, x1_ready)
                if m:
                    wait(m, m_ready)
                    wait(m, e_ready, 1)
                    eng.tensor_tensor(s_m[:, :, :].rearrange("p u (i j) -> p (u i) j", j=NH), sc,
                                      m_sb[:, :, :].rearrange("p u i -> p (u i)").unsqueeze(2).to_broadcast([P, 2 * NH, NH]),
                                      ALU.subtract).then_inc(sm_ready, 1)

                def divide(u):
                    wait(b, oraw_ready[u])
                    wait(b, rden_ready)
                    wait(b, og_ready, 2)
                    ins = eng.tensor_tensor(o_n[:, b.slot(2), u, :, :].rearrange("p d i -> p i d"),
                                            o_raw[:, u, :].rearrange("p (i d) -> p i d", d=HD),
                                            r_den[:, b.slot(2), u, :].unsqueeze(2).to_broadcast([P, NH, HD]), ALU.mult)
                    if u == 1:
                        ins.then_inc(on_ready, 1)

                if b:
                    wait(b, ev_ready[1])
                    eng.tensor_reduce(o_raw[:, 1, :], prod_ev[:, 1, :, :, :], AX.X, ALU.add).then_inc(oraw_ready[1], 1)
                    divide(0)
                if c:
                    s = c.slot(2)
                    wait(c, x1_ready)
                    wait(c, xq_ready, 1)
                    for u in range(2):
                        ins = eng.tensor_tensor(couples(xq_b[:, u, :]), swapped(x1[:, s, u, :]), couples(const("sq")), ALU.mult)
                    ins.then_inc(xqb_ready, 1)
                    eng.tensor_tensor(xq_a[:, :, :], x1[:, s, :, :], twice(const("cq")), ALU.mult).then_inc(xqa_ready, 1)
                if b:
                    divide(1)
                if c:
                    wait(c, xqa_ready)
                    wait(c, xqb_ready)
                    wait(c, kvp_ready[3], 1)
                    eng.tensor_tensor(xq[:, :, :], xq_a[:, :, :], xq_b[:, :, :], ALU.add).then_inc(xq_ready, 1)
                if e:
                    wait(e, ex_ready)
                    wait(e, w1_ready, 2)
                    eng.tensor_scalar(dn[:, e.slot(2), :], ex[:, e.slot(2), :], 1.0, None, ALU.add).then_inc(dn_ready, 1)
                if c:
                    wait(c, xq_ready)
                    wait(c, ret_ready, 1)
                    times_sums(0)
                if e:
                    wait(e, dn_ready)
                    eng.reciprocal(xe[:, e.slot(RING), :, 0, P], dn[:, e.slot(2), :]).then_inc(w1_ready, 1)
                if c:
                    times_sums(1)
                if e:
                    wait(e, w1_ready)
                    eng.tensor_tensor(xe[:, e.slot(RING), :, 1, P], ex[:, e.slot(2), :], xe[:, e.slot(RING), :, 0, P],
                                      ALU.mult).then_inc(w2_ready, 1)
                if a:
                    wait(a, qkv_ready)
                    for u in range(2):
                        wait(a, score_done[u], 1)
                        q = qkv[:, a.slot(RING), u, 0:P].rearrange("p (d i) -> p d i", i=NH)
                        k = qkv[:, a.slot(RING), u, P:2 * P].rearrange("p (d j) -> p d j", j=NH)
                        eng.tensor_tensor(prod_qk[:, u, :, :].rearrange("p d (i j) -> p d i j", j=NH),
                                          q.unsqueeze(3).to_broadcast([P, HD, NH, NH]),
                                          k.unsqueeze(2).to_broadcast([P, HD, NH, NH]), ALU.mult).then_inc(qk_ready[u], 1)
                if e:
                    wait(e, rank_done)
                    wait(e, cnt_ready, 1)
                    wait(e, posw_ready, 1)
                    eng.tensor_tensor(posf[:, :, :], RANK[:, 0:2 * n_exp].rearrange("p (u e) -> p u e", u=2),
                                      twice(cnt[:, :]), ALU.add).then_inc(posf_ready, 1)
                if c:
                    times_sums(2)
                if e:
                    wait(e, posf_ready)
                    eng.tensor_tensor(cnt[:, :], RANK[:, 2 * n_exp:3 * n_exp], cnt[:, :], ALU.add).then_inc(cnt_ready, 1)
                    wait(e, pos_ready, 1)
                    eng.tensor_tensor(posw[:, :, :, :], oh[:, e.slot(2), :, :, :],
                                      posf[:, :, :].unsqueeze(2).to_broadcast([P, 2, 2, n_exp]), ALU.mult).then_inc(posw_ready, 1)
                if c:
                    times_sums(3)
                if e:
                    wait(e, posw_ready)
                    wait_ring(e, routed_out, RING, 64)
                    with nc.allow_low_precision(reason="whole numbers below 2**24"):
                        eng.tensor_reduce(pos[:, e.slot(RING), :], posw[:, :, :, :].rearrange("p u k e -> p (u k) e"),
                                          AX.X, ALU.add).then_inc(pos_ready, 1)
                if y:
                    s = y.slot(2)
                    wait(y, y_done)
                    wait_ring(y, x_res_in)
                    wait(y, x1_ready, 2)
                    eng.tensor_tensor(res1[:, s, :, :], Y.rearrange("p (u c) -> p u c", u=2), x_res[:, y.slot(RING), :, :],
                                      ALU.add).then_inc(res1_ready, 1)

                def sum_dims(u):
                    wait(c, kvp_ready[2 * u])
                    wait(c, kvp_ready[2 * u + 1])
                    wait(c, res2_ready, 1)
                    ins = eng.tensor_reduce(ret[:, u, :], prod_kv[:, u, :].rearrange("p (d i) -> p d i", i=HD), AX.X, ALU.add)
                    if u == 1:
                        ins.then_inc(ret_ready, 1)

                if c:
                    sum_dims(0)
                if y:
                    spread(y, res1, stat1, res1_ready, stat1_ready, mv1_ready)
                if c:
                    sum_dims(1)
                if y:
                    moments(y, 0, stat1, mv1, stat1_ready, mv1_ready, nb1_ready)
                if d:
                    wait(d, logit_done)
                    wait(d, ix_ready, 2)
                    eng.tensor_copy(lg[:, d.slot(2), :, :].rearrange("p u e -> p (u e)"), LG).then_inc(lg_ready, 1)
                if c:
                    s = c.slot(2)
                    wait(c, ret_ready)
                    wait(c, x2_ready, 2)
                    eng.tensor_tensor(res2[:, s, :, :], ret[:, :, :], x1[:, s, :, :], ALU.add).then_inc(res2_ready, 1)
                if d:
                    wait(d, lg_ready)
                    wait(d, dlt_ready, 2)
                    stand(d, 2)
                    for u in range(2):
                        ins = eng.max(mx8[:, d.slot(2), u, :], lg[:, d.slot(2), u, :])
                    ins.then_inc(mx_ready, 1)
                if c:
                    spread(c, res2, stat2, res2_ready, stat2_ready, mv2_ready)
                if d:
                    s = d.slot(2)
                    wait(d, mx_ready)
                    wait(d, ex_ready, 2)
                    eng.tensor_tensor(dlt[:, s, :], mx8[:, s, :, 1], mx8[:, s, :, 0], ALU.subtract).then_inc(dlt_ready, 1)
                    for u in range(2):
                        ins = eng.max_index(ix8[:, s, u, :], mx8[:, s, u, :], lg[:, s, u, :])
                    ins.then_inc(ix_ready, 1)
                if c:
                    moments(c, 1, stat2, mv2, stat2_ready, mv2_ready, nb2_ready)
                if m:
                    wait(m, e_ready)
                    wait(m, rden_ready, 1)
                    eng.tensor_reduce(den[:, :, :].rearrange("p u i -> p (u i)"),
                                      e_sb[:, m.slot(2), :, :].rearrange("p u (i j) -> p (u i) j", j=NH), AX.X,
                                      ALU.add).then_inc(den_ready, 1)
                if d:
                    s = d.slot(2)
                    wait(d, ix_ready)
                    wait(d, posw_ready, 2)
                    for u in range(2):
                        ins = eng.tensor_tensor(oh[:, s, u, :, :], twice(const("iota_e")),
                                                ix8[:, s, u, 0:2].unsqueeze(2).to_broadcast([P, 2, n_exp]), ALU.is_equal)
                    ins.then_inc(oh_ready, 1)
                if m:
                    wait(m, den_ready)
                    wait(m, on_ready, 2)
                    eng.reciprocal(r_den[:, m.slot(2), :, :], den[:, :, :]).then_inc(rden_ready, 1)
                if d:
                    wait(d, oh_ready)
                    wait(d, rank_done, 2)
                    eng.tensor_tensor(ohs[:, s, :, :], oh[:, s, :, 0, :], oh[:, s, :, 1, :], ALU.add).then_inc(ohs_ready, 1)

            run_steps(eng, n_duo, A_FIRST, A_LAGS, step)

            links = [0]

            def link(ins):
                links[0] += 1
                ins.then_inc(chain, 1)
                eng.wait_ge(chain, links[0])

            eng.wait_ge(cnt_ready, n_duo)
            link(eng.tensor_scalar(pad_f[:, :], cnt[:, :], const("lane"), None, ALU.add))
            eng.wait_ge(oraw_ready[1], n_duo)
            eng.memset(pads[:, :, 0:P + 1], 0.0)
            eng.tensor_copy(pads[:, :, P + 1], const("spare_ids"))
            eng.tensor_copy(pad_i[:, :], pad_f[:, :]).then_inc(padi_ready, 1)
            one = slice(0, 1)
            link(eng.tensor_tensor(c_cnt[one, :], cnt[one, :], const("base_e")[one, :], ALU.subtract))
            link(eng.tensor_scalar(c_int[one, :], c_cnt[one, :], float(P - 1), None, ALU.add))
            link(eng.tensor_scalar(c_sh[one, :], c_int[one, :], 7, None, ALU.logical_shift_right))
            link(eng.tensor_copy(n_t[one, :], c_sh[one, :]))
            link(eng.tensor_copy(cum[one, 0:1], n_t[one, 0:1]))
            for n in range(1, n_exp):
                link(eng.tensor_tensor(cum[one, n:n + 1], cum[one, n - 1:n], n_t[one, n:n + 1], ALU.add))
            eng.memset(t_exp[one, :], 0.0)
            link(eng.memset(t_prev[one, :], 0.0))
            no = const("tile_no")[one, :]
            for n in range(n_exp - 1):
                link(eng.tensor_scalar(t_ge[one, :], no, cum[one, n:n + 1], None, ALU.is_ge))
                link(eng.tensor_tensor(t_exp[one, :], t_exp[one, :], t_ge[one, :], ALU.add))
                link(eng.scalar_tensor_tensor(out=t_prev[one, :], in0=t_ge[one, :], scalar=n_t[one, n:n + 1],
                                              in1=t_prev[one, :], op0=ALU.mult, op1=ALU.add))
            link(eng.tensor_tensor(t_prev[one, :], no, t_prev[one, :], ALU.subtract))
            link(eng.tensor_scalar(t_base[one, :], t_exp[one, :], float(region), None, ALU.mult))
            link(eng.scalar_tensor_tensor(out=t_base[one, :], in0=t_prev[one, :], scalar=float(P), in1=t_base[one, :],
                                          op0=ALU.mult, op1=ALU.add))
            link(eng.tensor_scalar(t_ge[one, :], no, cum[one, n_exp - 1:n_exp], None, ALU.is_ge))
            link(eng.tensor_scalar(t_dif[one, :], no, float(P), float(n_exp * region - P * (n_tiles - n_exp)), ALU.mult, ALU.add))
            link(eng.tensor_tensor(t_dif[one, :], t_dif[one, :], t_base[one, :], ALU.subtract))
            link(eng.tensor_tensor(t_dif[one, :], t_dif[one, :], t_ge[one, :], ALU.mult))
            link(eng.tensor_tensor(t_base[one, :], t_base[one, :], t_dif[one, :], ALU.add))
            link(eng.tensor_copy(tile_base[one, :], t_base[one, :]))
            eng.tensor_copy(tile_exp[one, :], t_exp[one, :]).then_inc(table_ready, 1)

            U = [KV[:, 0:512], KV[:, 512:1024]]

            def tile_step(at):
                if t := at(1):
                    wait(t, u_done)
                    wait(t, sil_ready)
                    wait(t, ht_done, 2)
                    eng.tensor_tensor(hid[:, t.slot(2), :], U[t.slot(2)], sil[:, t.slot(2), :], ALU.mult).then_inc(hid_ready, 1)
                if t := at(2):
                    s = t.slot(RING)
                    wait(t, down_done)
                    wait(t, xh_ready)
                    wait_ring(t, half_out, RING)
                    eng.scalar_tensor_tensor(out=yw[:, s, :], in0=YY[:, 0:P], scalar=xg[:, s, P:P + 1], in1=xh[:, t.slot(2), :],
                                             op0=ALU.mult, op1=ALU.add).then_inc(yw_ready, 1)
                    eng.tensor_copy(tok_i[:, s, :], xg[:, s, P + 1:ROW]).then_inc(tok_ready, 1)

            run_steps(eng, n_tiles, B_FIRST, B_LAGS, tile_step)

            def last_norm(at):
                if c := at(1):
                    s = c.slot(2)
                    wait(c, fsum_ready)
                    wait(c, fmv_ready, 2)
                    for n in range(C_SLICES):
                        ins = eng.bn_stats(fstat[:, s, n, :], fin[:, c.slot(RING), n, 0, :])
                    ins.then_inc(fstat_ready, 1)
                    wait(c, fstat_ready)
                    wait(c, fout_ready, 2)
                    stand(c, 3)
                    for n in range(C_SLICES):
                        ins = eng.bn_aggr(fmv[:, s, n, :], fstat[:, s, n, :])
                    ins.then_inc(fmv_ready, 1)
                if c := at(2):
                    s = c.slot(2)
                    wait(c, frs_ready)
                    for n in range(C_SLICES):
                        y = fin[:, c.slot(RING), n, 0, :]
                        ins = eng.tensor_scalar(y, y, fmv[:, s, n, 0:1], frs[:, s, n:n + 1], ALU.subtract, ALU.mult)
                    ins.then_inc(fout_ready, 1)

            run_steps(eng, n_chunks_c, C_FIRST, C_LAGS, last_norm)

        @block.gpsimd
        def _(eng):
            eng.memset(eps_c[:, :], EPS)
            eng.memset(half_c[:, :], -0.5).then_inc(pool_consts, 1)
            eng.wait_ge(pool_consts, 1)
            eng.wait_ge(tab_in, 16)

            def rstd(it, mv, ve, rs, mv_ready, ve_ready, rs_ready, used):
                s = it.slot(2)
                wait(it, mv_ready)
                wait(it, rs_ready, 2)
                eng.tensor_tensor(ve[:, s, :], mv[:, s, :, 1], eps_c[:, 0:2], ALU.add).then_inc(ve_ready, 1)
                wait(it, ve_ready)
                wait(it, used, 2)
                eng.tensor_tensor(rs[:, s, :], ve[:, s, :], half_c[:, 0:2], ALU.pow).then_inc(rs_ready, 1)

            def step(at):
                a, b, c, d, e = (at(lag) for lag in (3, 5, 6, 7, 8))
                if d:
                    rstd(d, mv2, ve2, rs2, mv2_ready, ve2_ready, rs2_ready, x2_ready)
                if c:
                    rstd(c, mv1, ve1, rs1, mv1_ready, ve1_ready, rs1_ready, x1_ready)
                if b:
                    wait_ring(b, ctx_in)
                    cs = ctx_sb[:, b.slot(RING), :, :]
                    wait(b, xk_ready, 1)
                    eng.tensor_tensor(xk_a[:, :, :], cs, twice(const("ck")), ALU.mult).then_inc(xka_ready, 1)
                    for u in range(2):
                        ins = eng.tensor_tensor(couples(xk_b[:, u, :]), swapped(cs[:, u, :]), couples(const("sk")), ALU.mult)
                    ins.then_inc(xkb_ready, 1)
                    wait(b, xka_ready)
                    wait(b, xkb_ready)
                    wait(b, kv_ready, 1)
                    eng.tensor_tensor(xk[:, :, :], xk_a[:, :, :], xk_b[:, :, :], ALU.add).then_inc(xk_ready, 1)
                    wait(b, xk_ready)
                    wait(b, kv_done[3], 2)
                    for u in range(2):
                        ins = eng.tensor_tensor(
                            kv[:, b.slot(2), u, :].rearrange("p (h j i) -> p h j i", j=HD, i=HD),
                            xk[:, u, :].rearrange("p (h i) -> p h i", i=HD).unsqueeze(2).to_broadcast([P, NH, HD, HD]),
                            cs[:, u, :].rearrange("p (h j) -> p h j", j=HD).unsqueeze(3).to_broadcast([P, NH, HD, HD]),
                            ALU.mult)
                    ins.then_inc(kv_ready, 1)
                if a:
                    s = a.slot(2)
                    wait(a, e_ready)
                    for u in range(2):
                        wait(a, oraw_ready[u], 1)
                        eng.tensor_tensor(
                            prod_ev[:, u, :, :, :],
                            e_sb[:, s, u, :].rearrange("p (i j) -> p i j", j=NH).unsqueeze(2).to_broadcast([P, NH, HD, NH]),
                            qkv[:, a.slot(RING), u, 2 * P:3 * P].rearrange("p (d j) -> p d j", j=NH).unsqueeze(1).to_broadcast([P, NH, HD, NH]),
                            ALU.mult).then_inc(ev_ready[u], 1)
                if e:
                    r = e.slot(RING)
                    wait(e, w2_ready)
                    eng.tensor_copy(xe[:, r, :, :, P + 1],
                                    const("ids")[:, bass.ds(e.number() * 4, 4)].rearrange("p (u k) -> p u k", k=2)
                                    ).then_inc(id_ready, 1)
                    wait(e, pos_ready)
                    wait(e, id_ready)
                    stand(e, 4)
                    for n in range(4):
                        eng.indirect_dma_start(out=xs, out_offset=bass.IndirectOffsetOnAxis(ap=pos[:, r, n:n + 1], axis=0),
                                               in_=xe[:, r, n // 2, n % 2, :], in_offset=None).then_inc(routed_out[r], 16)

            run_steps(eng, n_duo, A_FIRST, A_LAGS, step)

            eng.wait_ge(padi_ready, 1)
            for n in range(n_exp):
                eng.indirect_dma_start(out=xs, out_offset=bass.IndirectOffsetOnAxis(ap=pad_i[:, n:n + 1], axis=0),
                                       in_=pads[:, n, :], in_offset=None).then_inc(pads_out, 16)
            eng.dma_start(xs[n_exp * region:n_exp * (region + P), :].rearrange("(n p) c -> p n c", p=P),
                          pads[:, n_exp:2 * n_exp, :]).then_inc(pads_out, 16)

            def scatter_tile(at):
                if t := at(3):
                    s = t.slot(RING)
                    wait(t, yw_ready)
                    wait(t, tok_ready)
                    stand(t, 5)
                    eng.indirect_dma_start(out=halves, out_offset=bass.IndirectOffsetOnAxis(ap=tok_i[:, s, :], axis=0),
                                           in_=yw[:, s, :], in_offset=None).then_inc(half_out[s], 16)

            run_steps(eng, n_tiles, B_FIRST, B_LAGS, scatter_tile)

            def last_norm(at):
                if c := at(0):
                    wait_ring(c, fin_in)
                    y = fin[:, c.slot(RING), :, :, :]
                    eng.tensor_tensor(y[:, :, 0, :], y[:, :, 0, :], y[:, :, 1, :], ALU.add).then_inc(fsum_ready, 1)
                if c := at(1):
                    s = c.slot(2)
                    wait(c, fmv_ready)
                    wait(c, frs_ready, 2)
                    eng.tensor_tensor(fve[:, s, :], fmv[:, s, :, 1], eps_c[:, 0:C_SLICES], ALU.add).then_inc(fve_ready, 1)
                    wait(c, fve_ready)
                    wait(c, fout_ready, 2)
                    eng.tensor_tensor(frs[:, s, :], fve[:, s, :], half_c[:, 0:C_SLICES], ALU.pow).then_inc(frs_ready, 1)

            run_steps(eng, n_chunks_c, C_FIRST, C_LAGS, last_norm)


def kernel(x, ctx_1024, L0_attn_Wq, L0_attn_Wk, L0_attn_Wv, L0_attn_Wo, L0_attn_bo, L0_ffn_gate,
           L0_ffn_experts_w1, L0_ffn_experts_w2, L0_ffn_experts_w3):
    import concourse.bacc as bacc
    from concourse.bass_utils import run_bass_kernel_spmd

    shape = x.shape
    n_tok = shape[0] * shape[1]
    n_exp = L0_ffn_experts_w1.shape[0]
    table, where = constants(n_tok, n_exp)
    by_dim = np.arange(P).reshape(NH, HD).T.ravel()
    w_qkv = [np.asarray(w).T[:, by_dim] for w in (L0_attn_Wq, L0_attn_Wk, L0_attn_Wv)]
    wo = np.asarray(L0_attn_Wo).T.reshape(NH, HD, P)
    arrays = {
        "x": np.asarray(x).reshape(n_tok, P),
        "ctx": np.asarray(ctx_1024).reshape(n_tok, P),
        "w_qkv": np.concatenate(w_qkv, 1),
        "wo_by_token": np.ascontiguousarray(wo[np.arange(P) % NH]),
        "bo": np.asarray(L0_attn_bo).reshape(P, 1),
        "gate": np.asarray(L0_ffn_gate),
        "w1": np.asarray(L0_ffn_experts_w1),
        "w3": np.asarray(L0_ffn_experts_w3),
        "w2": np.asarray(L0_ffn_experts_w2),
        "table": table,
    }
    nc = bacc.Bacc("TRN2", target_bir_lowering=False, num_devices=1)
    aps = {n: nc.dram_tensor(n, a.shape, mybir.dt.from_np(a.dtype), kind="ExternalInput").ap() for n, a in arrays.items()}
    out = nc.dram_tensor("out", (n_tok, P), F32, kind="ExternalOutput").ap()
    build(nc, **aps, where=where, out=out)
    result = run_bass_kernel_spmd(nc, [arrays], core_ids=[0])
    return result.results[0]["out"].reshape(shape)
```

```python
from contextlib import ExitStack

import numpy as np

import concourse.bass as bass
from concourse import mybir
from concourse.alu_op_type import AluOpType as ALU

ACT = mybir.ActivationFunctionType
AX = mybir.AxisListType
F32 = mybir.dt.float32
F16 = mybir.dt.float16
BF16 = mybir.dt.bfloat16
I32 = mybir.dt.int32
U32 = mybir.dt.uint32

P = 128
S = 64
NH = 16
HD = 8
UNROLL = 4
RING = 4
TILE = 2 * P
ROW = P + 2
EPS = 1e-5
X_SCALE = 2.0 ** 8
W_SCALE = 2.0 ** 14
H_BOUND = 2.0 ** 15
TINY = 1e-15


def constants(n_tok, n_exp):
    p = np.arange(P)
    b, t = p // S, p % S
    d = np.arange(P)
    head, r = d // HD, d % HD
    e = r // 2
    gam = 1.0 - np.exp(np.linspace(np.log(1.0 / 32.0), np.log(1.0 / 512.0), P // HD))
    base = (2.0 * np.arange(HD // 2) + 0.4 * HD) / (1.4 * HD)
    inv = 1.0 / 10000.0 ** (np.arange(HD // 2) / (HD // 2))
    ang = t[:, None] * inv[e][None, :]
    scale = base[e][None, :] ** (t[:, None] / 512.0)
    decay = gam[head][None, :] ** t[:, None]
    sign = np.where(r % 2 == 0, -1.0, 1.0)[None, :]
    same = b[:, None] == b[None, :]
    parts = {
        "ident": np.eye(P),
        "minus": -np.eye(P),
        "tri": same & (t[:, None] <= t[None, :]),
        "before": p[:, None] < p[None, :],
        "group": p[:, None] // NH == np.arange(P // NH),
        "cq": np.cos(ang) * scale * decay,
        "sq": np.sin(ang) * scale * decay * sign,
        "ck": np.cos(ang) / scale / decay,
        "sk": np.sin(ang) / scale / decay * sign,
        "iota_e": np.broadcast_to(np.arange(n_exp), (P, n_exp)),
        "base_e": np.broadcast_to(np.arange(n_exp) * (n_tok + TILE), (P, n_exp)),
        "spare_ids": 2 * n_tok + p[:, None] + P * np.arange(4 * n_exp)[None, :],
        "ids": 2 * p[:, None] + 2 * P * (np.arange(2 * n_tok // P) // 2) + np.arange(2 * n_tok // P) % 2,
        "tile_no": np.broadcast_to(np.arange(2 * n_tok // TILE + n_exp), (P, 2 * n_tok // TILE + n_exp)),
    }
    where, at = {}, 0
    for name, a in parts.items():
        n = int(np.prod(a.shape[1:]))
        where[name] = (at, at + n)
        at += n
    table = np.concatenate([np.asarray(a, np.float64).reshape(P, -1) for a in parts.values()], 1)
    return table.astype(np.float32), where


class Item:

    def __init__(self, eng, i, snaps, off):
        self.eng, self.i, self.snaps, self.off = eng, i, snaps, off

    def slot(self, n):
        return self.off % n

    def number(self, lo=0, hi=None):
        return self.off if self.i is None else self.i * UNROLL + self.off

    def count(self, back=0):
        n = self.off + 1 - back
        if self.i is None:
            return n
        assert n > 0
        key = (UNROLL, n)
        if key not in self.snaps:
            self.snaps[key] = self.eng.snap(self.i * UNROLL + n)
        return self.snaps[key]

    def ring_count(self, per, back=0):
        n = (self.off - back) // RING + 1
        if self.i is None:
            return per * n
        assert n > 0
        key = (per, n)
        if key not in self.snaps:
            self.snaps[key] = self.eng.snap((self.i + n) * per)
        return self.snaps[key]


def wait(item, sem, back=0):
    if item.i is None and item.off + 1 - back <= 0:
        return
    item.eng.wait_ge(sem, item.count(back))


def wait_ring(item, sems, back=0, per=16):
    if item.i is None and item.off - back < 0:
        return
    item.eng.wait_ge(sems[(item.off - back) % RING], item.ring_count(per, back))


def run_steps(eng, n, first, lags, body):
    def alone(s):
        body(lambda lag: Item(eng, None, None, s - lag) if 0 <= s - lag < n else None)

    for s in range(first):
        alone(s)
    if n > first:
        with eng.Fori(0, (n - first) // UNROLL) as i:
            snaps = {}
            for k in range(UNROLL):
                body(lambda lag, k=k: Item(eng, i, snaps, first + k - lag))
    for s in range(n, n + lags):
        alone(s)


def build(nc, x, ctx, w_qkv, wo_by_token, bo, gate, w1, w3, w2, table, where, out):
    n_tok = x.shape[0]
    n_exp, inner = w1.shape[0], w1.shape[2]
    n_chunk = inner // P
    n_duo = n_tok // (2 * P)
    region = n_tok + TILE
    n_tiles = 2 * n_tok // TILE + n_exp
    A_FIRST, A_LAGS = 12, 8
    B_FIRST, B_LAGS = 8, 3
    C_SLICES = 4
    n_chunks_c = n_tok // P // C_SLICES
    C_FIRST, C_LAGS = 8, 3
    assert (n_duo - A_FIRST) % UNROLL == 0 and (n_tiles - B_FIRST) % UNROLL == 0

    xs = nc.dram_tensor("routed_rows", [n_exp * (region + TILE), ROW], F32).ap()
    halves = nc.dram_tensor("token_halves", [2 * n_tok + 2 * n_exp * TILE, P], F32).ap()

    x_duos = x.rearrange("(n u p) d -> n p u d", u=2, p=P)
    ctx_duos = ctx.rearrange("(n u p) d -> n p u d", u=2, p=P)
    half_rows = halves[0:2 * n_tok, :].rearrange("(p n k) d -> p n k d", p=P, k=2)
    out_rows = out.rearrange("(p n) d -> p n d", p=P)

    with ExitStack() as stack:
        def sb(name, shape, dt=F32):
            return stack.enter_context(nc.sbuf_tensor(name, [P, *shape], dt))

        def ps(name, n):
            return stack.enter_context(nc.psum_tensor(name, [P, n], F32))

        def sem(name):
            return stack.enter_context(nc.semaphore(name))

        def ring_sem(name):
            return [sem(f"{name}{i}") for i in range(RING)]

        tab = sb("tab", [table.shape[1]])

        def const(name):
            a, b = where[name]
            return tab[:, a:b]

        ident, minus, tri = const("ident"), const("minus"), const("tri")
        w_qkv_sb = sb("w_qkv_sb", [3 * P])
        wo_sb = sb("wo_sb", [HD, P])
        bo_sb = sb("bo_sb", [1])
        gate_sb = sb("gate_sb", [n_exp])
        w_new = sb("w_new", [n_exp * inner])
        w1_hl, w3_hl, w2_hl = (sb(n, [2, n_exp * inner], F16) for n in ("w1_hl", "w3_hl", "w2_hl"))
        w_high, w_max, w_top, w_inv, w_scale = (sb(n, [3]) for n in ("w_high", "w_max", "w_top", "w_inv", "w_scale"))
        w_mats = sb("w_mats", [P])
        silu_scale, hid_scale, top13, y_scale = (sb(n, [1]) for n in ("silu_scale", "hid_scale", "top13", "y_scale"))
        before_bf = sb("before_bf", [P], BF16)
        ones_bf = sb("ones_bf", [P], BF16)
        eps_c = sb("eps_c", [8])
        half_c = sb("half_c", [8])

        x_sb, x_res, ctx_sb = (sb(n, [RING, 2, P]) for n in ("x_sb", "x_res", "ctx_sb"))
        x_t = sb("x_t", [2, 2, P])
        qkv = sb("qkv", [RING, 2, 3 * P])
        prod_qk = sb("prod_qk", [2, HD, NH * NH])
        m_sb = sb("m_sb", [2, NH])
        e_sb = sb("e_sb", [2, 2, NH * NH])
        den, r_den = sb("den", [2, NH]), sb("r_den", [2, 2, NH])
        prod_ev = sb("prod_ev", [2, NH, HD, NH])
        o_raw = sb("o_raw", [2, P])
        o_n = sb("o_n", [2, 2, HD, NH])
        o_g = sb("o_g", [2, HD, HD, NH])
        y_t = sb("y_t", [2, P])
        res1, res2 = sb("res1", [2, 2, P]), sb("res2", [2, 2, P])
        stat1, stat2 = sb("stat1", [2, 2, 6]), sb("stat2", [2, 2, 6])
        mv = sb("mv", [2, 2, 2, 2])
        ve, rs, nb = (sb(n, [2, 2, 2]) for n in ("ve", "rs", "nb"))
        x1 = sb("x1", [2, 2, P])
        xq_a, xq_b, xq = sb("xq_a", [2, P]), sb("xq_b", [2, P]), sb("xq", [2, P])
        xk_a, xk_b, xk = sb("xk_a", [2, P]), sb("xk_b", [2, P]), sb("xk", [2, P])
        kv = sb("kv", [2, 2, 1024])
        prod_kv = sb("prod_kv", [2, 1024])
        ret = sb("ret", [2, P])
        xe = sb("xe", [RING, 2, 2, ROW])
        x2_t = sb("x2_t", [2, 2, P])
        lg = sb("lg", [2, 2, n_exp])
        mx8, ix8 = sb("mx8", [2, 2, 8]), sb("ix8", [2, 2, 8], U32)
        dlt, ex, dn = sb("dlt", [2, 2]), sb("ex", [2, 2]), sb("dn", [2, 2])
        oh = sb("oh", [2, 2, 2, n_exp])
        ohs = sb("ohs", [2, 2, n_exp], BF16)
        cnt = sb("cnt", [n_exp])
        posf, posw = sb("posf", [2, n_exp]), sb("posw", [2, 2, n_exp])
        pos = sb("pos", [RING, 4], I32)

        pad_i = sb("pad_i", [n_exp], I32)
        c_cnt, c_int, c_sh = sb("c_cnt", [n_exp]), sb("c_int", [n_exp], I32), sb("c_sh", [n_exp], I32)
        n_t, cum = sb("n_t", [n_exp]), sb("cum", [n_exp])
        t_ge, t_exp, t_prev, t_base, t_dif = (sb(n, [n_tiles]) for n in ("t_ge", "t_exp", "t_prev", "t_base", "t_dif"))
        tile_exp, two_exp, tile_base = (sb(n, [n_tiles], I32) for n in ("tile_exp", "two_exp", "tile_base"))

        def zero_rows(ap):
            return ap[:, 0:2 * n_exp * ROW].rearrange("p (n c) -> p n c", c=ROW)

        spare_rows = zero_rows(prod_ev[:, :, :, :, :].rearrange("p u i d j -> p (u i d j)"))
        pad_rows = zero_rows(w_new)

        def in_new(at, c):
            return w_new[:, at * RING * 2:(at + c) * RING * 2].rearrange("p (r u c) -> p r u c", r=RING, u=2)

        xg, yw, xh = in_new(0, ROW), in_new(ROW, P), in_new(ROW + P, P)
        x_hl = sb("x_hl", [2, 2, TILE], F16)
        wt = sb("wt", [RING, 2])
        stage_b = prod_qk[:, :, :, :].rearrange("p u d i -> p (u d i)")
        stage_b2 = prod_ev[:, :, :, :, :].rearrange("p u i d j -> p (u i d j)")
        sil, hid = (stage_b[:, n * 4 * inner:(n + 1) * 4 * inner].rearrange("p (s i) -> p s i", s=2) for n in range(2))
        hid_hi, hid_lo = (stage_b2[:, 2 * n * inner:2 * (n + 1) * inner].bitcast(F16).rearrange("p (s i) -> p s i", s=2)
                          for n in range(2))
        tok_i = sb("tok_i", [RING, 2], I32)

        fin = stage_b2.rearrange("p (r n k d) -> p r n k d", r=RING, n=C_SLICES, k=2)
        fout = stage_b[:, 0:RING * C_SLICES * P].rearrange("p (r n d) -> p r n d", r=RING, n=C_SLICES)
        fstat, fmv = sb("fstat", [2, C_SLICES, 6]), sb("fmv", [2, C_SLICES, 2])
        fve, frs, fnb = (sb(n, [2, C_SLICES]) for n in ("fve", "frs", "fnb"))

        XT, SC, YY, TR = ps("XT", 512), ps("SC", 512), ps("YY", 512), ps("TR", 512)
        QKV, KV = ps("QKV", 1024), ps("KV", 1024)
        qkv_ps = QKV[:, :].rearrange("p (u c) -> p u c", u=2)[:, :, 0:3 * P]
        YT, Y = YY[:, 0:2 * P], YY[:, 2 * P:4 * P]
        X2T, LG, RANK = TR[:, 0:2 * P], TR[:, 256:256 + 2 * n_exp], XT[:, 256:256 + 3 * n_exp]

        tab_in, small_in = sem("tab_in"), sem("small_in")
        abs_ready = sem("abs_ready")
        w_in = [sem(f"w_in{n}") for n in range(3)]
        max_ready, mats_ready, max_spread, top_ready, top_kept, inv_ready, scale_ready, hi_ready, lo_ready, exp_scales = (
            sem(n) for n in ("max_ready", "mats_ready", "max_spread", "top_ready", "top_kept", "inv_ready", "scale_ready",
                             "hi_ready", "lo_ready", "exp_scales"))
        consts_ready, pool_consts = sem("consts_ready"), sem("pool_consts")
        xt_done, qkv_done, x2t_done, logit_done, yt_done, y_done, rank_done = (
            sem(n) for n in ("xt_done", "qkv_done", "x2t_done", "logit_done", "yt_done", "y_done",
                             "rank_done"))
        score_done = [sem(f"score_done{u}") for u in range(2)]
        oraw_ready = [sem(f"oraw_ready{u}") for u in range(2)]
        sub_done = sem("sub_done")
        kv_done = [sem(f"kv_done{n}") for n in range(4)]
        xt_ready, qkv_ready, e_ready, og_ready, yt_ready, x2t_ready, ex_ready = (
            sem(n) for n in ("xt_ready", "qkv_ready", "e_ready", "og_ready", "yt_ready", "x2t_ready", "ex_ready"))
        qk_ready = [sem(f"qk_ready{u}") for u in range(2)]
        kvp_ready = [sem(f"kvp_ready{n}") for n in range(4)]
        m_ready, den_ready, rden_ready, on_ready = (
            sem(n) for n in ("m_ready", "den_ready", "rden_ready", "on_ready"))
        lg_ready, mx_ready, ix_ready, oh_ready, ohs_ready, dlt_ready = (
            sem(n) for n in ("lg_ready", "mx_ready", "ix_ready", "oh_ready", "ohs_ready", "dlt_ready"))
        res2_ready, stat2_ready, mv2_ready, res1_ready, stat1_ready, mv1_ready, ret_ready = (
            sem(n) for n in ("res2_ready", "stat2_ready", "mv2_ready", "res1_ready", "stat1_ready", "mv1_ready",
                             "ret_ready"))
        nb_ready, x1_ready, x2_ready, dn_ready, w1_ready, w2_ready = (
            sem(n) for n in ("nb_ready", "x1_ready", "x2_ready", "dn_ready", "w1_ready", "w2_ready"))
        xqa_ready, xqb_ready, xq_ready = (sem(n) for n in ("xqa_ready", "xqb_ready", "xq_ready"))
        posf_ready, cnt_ready, posw_ready, pos_ready = (
            sem(n) for n in ("posf_ready", "cnt_ready", "posw_ready", "pos_ready"))
        xka_ready, xkb_ready, xk_ready, kv_ready, id_ready = (
            sem(n) for n in ("xka_ready", "xkb_ready", "xk_ready", "kv_ready", "id_ready"))
        ev_ready = [sem(f"ev_ready{u}") for u in range(2)]
        ve_ready, rs_ready = sem("ve_ready"), sem("rs_ready")
        x_in, x_res_in, ctx_in, routed_out = (ring_sem(n) for n in ("x_in", "x_res_in", "ctx_in", "routed_out"))
        chain, padi_ready, table_ready, pads_out = sem("chain"), sem("padi_ready"), sem("table_ready"), sem("pads_out")
        spare_ready, spare_out, pads_ready = sem("spare_ready"), sem("spare_out"), sem("pads_ready")
        xg_in, half_out = ring_sem("xg_in"), ring_sem("half_out")
        xgt_done, down_done = sem("xgt_done"), sem("down_done")
        g_done, u_done, sil_ready, hid_ready = (
            [sem(f"{n}{half}") for half in range(2)] for n in ("g_done", "u_done", "sil_ready", "hid_ready"))
        xhi_ready, xlo_ready, xh_ready, hhi_ready, hlo_ready = (
            sem(n) for n in ("xhi_ready", "xlo_ready", "xh_ready", "hhi_ready", "hlo_ready"))
        yw_ready, tok_ready, wt_ready = (sem(n) for n in ("yw_ready", "tok_ready", "wt_ready"))
        fin_in, fin_out = ring_sem("fin_in"), ring_sem("fin_out")
        fnb_ready = sem("fnb_ready")
        fsum_ready, fstat_ready, fmv_ready, fve_ready, frs_ready, fout_ready = (
            sem(n) for n in ("fsum_ready", "fstat_ready", "fmv_ready", "fve_ready", "frs_ready", "fout_ready"))

        marks = sb("marks", [6])
        marked = [sem(f"marked{n}") for n in range(6)]

        def stand(it, n):
            wait(it, marked[n], 1)
            if n < 4:
                it.eng.memset(marks[:, n:n + 1], 0.0).then_inc(marked[n], 1)
            else:
                it.eng.tensor_tensor(marks[:, n:n + 1], half_c[:, 0:1], half_c[:, 0:1], ALU.add).then_inc(marked[n], 1)

        def absolute(n):
            return (w1_hl, w3_hl, w2_hl)[n][:, :, :].rearrange("p k i -> p (k i)").bitcast(F32)

        def moments_slot(it, lag):
            return (it.off + lag) % 2

        def wait_norms(c, d, sem, back=0):
            if c:
                wait(c, sem, back)
            else:
                wait(d, sem, back - 1)

        def at_step(at, n):
            it = at(0)
            return it is not None and it.i is None and it.off == n

        MEASURE, SPREAD_MAX, SPLIT, FETCH = (2, 6, 9), (3, 7, 10), (4, 8, 11), (5, 9)
        SPREAD = QKV[:, 3 * P:4 * P]

        def swapped(ap):
            return couples(ap)[:, :, ::-1]

        def couples(ap):
            return ap.rearrange("p (e w) -> p e w", w=2)

        def twice(ap):
            return ap.unsqueeze(1).to_broadcast([P, 2, ap.shape[1]])

        block = stack.enter_context(nc.Block())

        @block.sync
        def _(eng):
            eng.dma_start(tab[:, :], table).then_inc(tab_in, 16)
            eng.dma_start(w_qkv_sb[:, :], w_qkv).then_inc(small_in, 16)
            eng.dma_start(wo_sb[:, :, :], wo_by_token).then_inc(small_in, 16)
            eng.dma_start(bo_sb[:, :], bo).then_inc(small_in, 16)
            eng.dma_start(gate_sb[:, :], gate).then_inc(small_in, 16)

            def step(at):
                if it := at(0):
                    wait(it, xt_done, RING)
                    eng.dma_start(x_sb[:, it.slot(RING), :, :], x_duos[it.number()]).then_inc(x_in[it.slot(RING)], 16)
                if it := at(3):
                    wait(it, y_done, RING)
                    eng.dma_start(x_res[:, it.slot(RING), :, :], x_duos[it.number()]).then_inc(x_res_in[it.slot(RING)], 16)
                    wait(it, kv_ready, RING)
                    wait(it, xkb_ready, RING)
                    eng.dma_start(ctx_sb[:, it.slot(RING), :, :], ctx_duos[it.number()]).then_inc(ctx_in[it.slot(RING)], 16)

            run_steps(eng, n_duo, A_FIRST, A_LAGS, step)

            eng.wait_ge(pads_ready, 1)
            eng.wait_ge(padi_ready, 1)
            for n in range(n_exp // 2):
                row = eng.value_load(pad_i[0:1, n:n + 1], min_val=n * region, max_val=n * region + n_tok)
                eng.dma_start(xs[bass.ds(row, TILE), :].rearrange("(u p) c -> p u c", p=P),
                              pad_rows[:, 2 * n:2 * n + 2, :]).then_inc(pads_out, 16)

            for r in range(RING):
                eng.wait_ge(routed_out[r], 64 * n_duo // RING)
            eng.wait_ge(pads_out, 16 * n_exp)
            eng.wait_ge(spare_out, 16)
            eng.wait_ge(lo_ready, 3)
            eng.wait_ge(table_ready, 1)

            def load_tile(at):
                if t := at(0):
                    row = eng.value_load(tile_base[0:1, bass.ds(t.number(), 1)], min_val=0, max_val=(n_exp - 1) * TILE + n_exp * region)
                    wait(t, xgt_done, RING)
                    wait(t, xh_ready, RING)
                    wait(t, wt_ready, RING)
                    wait(t, tok_ready, RING)
                    eng.dma_start(xg[:, t.slot(RING), :, :],
                                  xs[bass.ds(row, TILE), :].rearrange("(u p) c -> p u c", p=P)).then_inc(xg_in[t.slot(RING)], 16)

            run_steps(eng, n_tiles, B_FIRST, 0, load_tile)

            for r in range(RING):
                eng.wait_ge(half_out[r], 32 * n_tiles // RING)

            def last_norm(at):
                if c := at(0):
                    wait(c, fout_ready, RING)
                    eng.dma_start(fin[:, c.slot(RING), :, :, :],
                                  half_rows[:, bass.ds(c.number() * C_SLICES, C_SLICES), :, :]).then_inc(fin_in[c.slot(RING)], 16)

            run_steps(eng, n_chunks_c, C_FIRST, 0, last_norm)

        @block.tensor
        def _(eng):
            eng.wait_ge(tab_in, 16)
            eng.wait_ge(small_in, 16 * 4)
            eng.wait_ge(consts_ready, 1)

            def step(at):
                z, a, m, y, c, d, e = (at(lag) for lag in (1, 2, 3, 5, 6, 7, 8))

                def kv_sums(n):
                    if n < 2:
                        wait(c, kvp_ready[n + 2], 1)
                    else:
                        wait(c, kvp_ready[n - 2])
                    eng.matmul(KV[:, 512 * (n % 2):512 * (n % 2) + 512], tri,
                               kv[:, c.slot(2), n // 2, 512 * (n % 2):512 * (n % 2) + 512],
                               start=True, stop=True).then_inc(kv_done[n], 1)

                def scores(it, u):
                    wait(it, qk_ready[u])
                    wait(it, e_ready, 1)
                    for n in range(HD):
                        mm = eng.matmul(SC[:, 256 * u:256 * u + 256], ident, prod_qk[:, u, n, :],
                                        start=(n == 0 and u == 0), stop=(n == HD - 1), skip_group_check=True)
                    mm.then_inc(score_done[u], 1)

                if m:
                    scores(m, 1)
                if c:
                    wait(c, kv_ready)
                    kv_sums(0)
                    kv_sums(1)
                if z:
                    wait_ring(z, x_in)
                    wait(z, xt_ready, 1)
                    wait(z, posf_ready, 8)
                    wait(z, cnt_ready, 8)
                    for u in range(2):
                        mm = eng.transpose(XT[:, P * u:P * u + P], x_sb[:, z.slot(RING), u, :], ident)
                    mm.then_inc(xt_done, 1)
                if m:
                    wait(m, m_ready)
                    eng.matmul(SC[:, :].rearrange("p (i j) -> p i j", j=NH), minus,
                               m_sb[:, :, :].rearrange("p u i -> p (u i)").unsqueeze(2).to_broadcast([P, 2 * NH, NH]),
                               start=False, stop=True, skip_group_check=True).then_inc(sub_done, 1)
                if y:
                    wait(y, og_ready)
                    wait(y, res1_ready, 1)
                    for n in range(HD):
                        mm = eng.matmul(YT, wo_sb[:, n, :], o_g[:, :, n, :, :].rearrange("p u g h -> p u (g h)"),
                                        start=(n == 0), stop=(n == HD - 1))
                    mm.then_inc(yt_done, 1)
                if d:
                    wait(d, x2_ready)
                    wait(d, lg_ready, 1)
                    for u in range(2):
                        mm = eng.transpose(X2T[:, P * u:P * u + P], xe[:, d.slot(RING), u, 0, 0:P], ident)
                    mm.then_inc(x2t_done, 1)
                if z:
                    wait(z, xt_ready)
                    wait(z, qkv_ready, 1)
                    for n in range(3):
                        if at_step(at, SPREAD_MAX[n] + 1):
                            eng.wait_ge(top_ready, n + 1)
                    for u in range(2):
                        mm = eng.matmul(qkv_ps[:, u, :], x_t[:, z.slot(2), u, :], w_qkv_sb[:, :], start=True, stop=True)
                    mm.then_inc(qkv_done, 1)
                if d:
                    wait(d, x2t_ready)
                    for u in range(2):
                        mm = eng.matmul(LG[:, n_exp * u:n_exp * u + n_exp], x2_t[:, d.slot(2), u, :], gate_sb[:, :],
                                        start=True, stop=True)
                    mm.then_inc(logit_done, 1)
                if c:
                    kv_sums(2)
                    kv_sums(3)
                if y:
                    wait(y, yt_ready)
                    wait_ring(y, x_res_in)
                    for u in range(2):
                        eng.matmul(Y[:, P * u:P * u + P], y_t[:, u, :], ident, start=True, stop=False)
                        mm = eng.matmul(Y[:, P * u:P * u + P], ident, x_res[:, y.slot(RING), u, :], start=False, stop=True)
                    mm.then_inc(y_done, 1)
                if e:
                    wait(e, ohs_ready)
                    o = ohs[:, e.slot(2), :, :]
                    eng.matmul(RANK[:, 0:2 * n_exp], before_bf[:, :], o.rearrange("p u e -> p (u e)"),
                               start=True, stop=False, skip_group_check=True)
                    eng.matmul(RANK[:, n_exp:2 * n_exp], ones_bf[:, :], o[:, 0, :], start=False, stop=True,
                               skip_group_check=True)
                    for u in range(2):
                        mm = eng.matmul(RANK[:, 2 * n_exp:3 * n_exp], ones_bf[:, :], o[:, u, :],
                                        start=(u == 0), stop=(u == 1), skip_group_check=True)
                    mm.then_inc(rank_done, 1)
                if a:
                    scores(a, 0)
                for n in range(3):
                    if at_step(at, SPREAD_MAX[n]):
                        eng.wait_ge(mats_ready, n + 1)
                        wait(z, qkv_ready)
                        eng.matmul(SPREAD, w_mats[:, :], ident, start=True, stop=True).then_inc(max_spread, 1)

            run_steps(eng, n_duo, A_FIRST, A_LAGS, step)

            eng.wait_ge(lo_ready, 3)
            eng.wait_ge(hi_ready, 3)
            eng.wait_ge(table_ready, 1)
            eng.wait_ge(pos_ready, n_duo)
            eng.wait_ge(res1_ready, n_duo)
            XGT, YB = [TR, YY], [XT, SC]

            def hidden_product(out, w_hl, no, x, half):
                for n in range(2):
                    for k, (wp, xp) in enumerate(((0, 0), (0, 1), (1, 0))):
                        mm = eng.matmul(out[:, 512 * half + TILE * n:512 * half + TILE * (n + 1)],
                                        w_hl[:, wp, bass.ds(no * inner + P * (2 * half + n), P)], x_hl[:, x, xp, :],
                                        start=(k == 0), stop=(k == 2))
                return mm

            def tile_step(at):
                t, up, down = at(0), at(1), at(3)
                if up and down:
                    both = eng.value_load(two_exp[0:1, bass.ds(up.number(), 1)], min_val=0, max_val=n_exp * n_exp - 1)
                    up_no, down_no = eng.snap(both // n_exp), eng.snap(both % n_exp)
                elif up or down:
                    up_no = down_no = eng.value_load(tile_exp[0:1, bass.ds((up or down).number(), 1)],
                                                     min_val=0, max_val=n_exp - 1)
                if t:
                    wait_ring(t, xg_in)
                    wait(t, xlo_ready, 2)
                    for u in range(2):
                        mm = eng.transpose(XGT[t.slot(2)][:, P * u:P * u + P], xg[:, t.slot(RING), u, 0:P], ident)
                    mm.then_inc(xgt_done, 1)
                if down:
                    wait(down, hhi_ready)
                    wait(down, hlo_ready)
                    wait(down, yw_ready, 2)
                    for u in range(2):
                        for n in range(n_chunk):
                            cols = bass.ds(down_no * inner + P * n, P)
                            for k, (h, wp) in enumerate(((hid_hi, 0), (hid_lo, 0), (hid_hi, 1))):
                                mm = eng.matmul(YB[down.slot(2)][:, P * u:P * u + P],
                                                h[:, down.slot(2), TILE * n + P * u:TILE * n + P * u + P], w2_hl[:, wp, cols],
                                                start=(n == 0 and k == 0), stop=(n == n_chunk - 1 and k == 2))
                    mm.then_inc(down_done, 1)
                if up:
                    wait(up, xhi_ready)
                    wait(up, xlo_ready)
                    for half in range(2):
                        wait(up, sil_ready[half], 1)
                        hidden_product(QKV, w1_hl, up_no, up.slot(2), half).then_inc(g_done[half], 1)
                        wait(up, hid_ready[half], 1)
                        hidden_product(KV, w3_hl, up_no, up.slot(2), half).then_inc(u_done[half], 1)

            run_steps(eng, n_tiles, B_FIRST, B_LAGS, tile_step)

        @block.scalar
        def _(eng):
            w2_parts = w2.rearrange("e (n p) h -> n p e h", p=P)

            def load_weights(n):
                if n > 0:
                    eng.wait_ge(lo_ready, n)
                if n < 2:
                    eng.dma_start(w_new[:, :].rearrange("p (e i) -> p e i", e=n_exp),
                                  (w1, w3)[n].rearrange("e h i -> h e i")).then_inc(w_in[n], 16)
                else:
                    for k in range(n_chunk):
                        eng.dma_start(w_new[:, :].rearrange("p (e n h) -> p e n h", e=n_exp, n=n_chunk)[:, :, k, :],
                                      w2_parts[k]).then_inc(w_in[n], 16)

            eng.wait_ge(tab_in, 16)
            eng.wait_ge(small_in, 16 * 4)

            def step(at):
                z, a, b, y, c, d = (at(lag) for lag in (1, 3, 4, 5, 6, 7))
                if at_step(at, 0):
                    load_weights(0)
                    eng.wait_ge(spare_ready, 1)
                    eng.dma_start(xs[n_exp * region:n_exp * (region + TILE), :].rearrange("(n p) c -> p n c", p=P),
                                  spare_rows).then_inc(spare_out, 16)

                for n in range(2):
                    if at_step(at, FETCH[n]):
                        load_weights(n + 1)
                for n in range(3):
                    if at_step(at, SPLIT[n]):
                        eng.wait_ge(scale_ready, n + 1)
                        eng.activation((w1_hl, w3_hl, w2_hl)[n][:, 0, :], w_new[:, :], ACT.Copy,
                                       scale=w_scale[:, n:n + 1]).then_inc(hi_ready, 1)
                if z:
                    wait(z, xt_done)
                    wait(z, qkv_done, 2)
                    eng.copy(x_t[:, z.slot(2), :, :].rearrange("p u t -> p (u t)"), XT[:, 0:2 * P]).then_inc(xt_ready, 1)
                if d:
                    s, r = d.slot(2), d.slot(RING)
                    wait(d, nb_ready, -1)
                    m = moments_slot(d, 6)
                    wait_ring(d, routed_out, RING, 64)
                    for u in range(2):
                        for k in range(2):
                            ins = eng.activation(xe[:, r, u, k, 0:P], res2[:, s, u, :], ACT.Identity,
                                                 bias=nb[:, m, 1, u:u + 1], scale=rs[:, m, 1, u:u + 1])
                    ins.then_inc(x2_ready, 1)
                if c:
                    s = c.slot(2)
                    wait(c, nb_ready)
                    m = moments_slot(c, 5)
                    wait(c, res2_ready, 2)
                    wait(c, xqb_ready, 2)
                    for u in range(2):
                        ins = eng.activation(x1[:, s, u, :], res1[:, s, u, :], ACT.Identity,
                                             bias=nb[:, m, 0, u:u + 1], scale=rs[:, m, 0, u:u + 1])
                    ins.then_inc(x1_ready, 1)
                if a:
                    wait(a, sub_done)
                    wait(a, ev_ready[1], 2)
                    wait(a, den_ready, 2)
                    eng.activation(e_sb[:, a.slot(2), :, :].rearrange("p u i -> p (u i)"), SC[:, :], ACT.Exp, scale=float(HD) ** -0.5).then_inc(e_ready, 1)
                if y:
                    wait(y, yt_done)
                    wait(y, y_done, 1)
                    for u in range(2):
                        ins = eng.activation(y_t[:, u, :].rearrange("p (b h g) -> p b g h", b=2, h=NH),
                                             YT[:, P * u:P * u + P].rearrange("p (b g h) -> p b g h", b=2, h=NH),
                                             ACT.Identity, bias=bo_sb[:, :])
                    ins.then_inc(yt_ready, 1)
                if d:
                    wait(d, x2t_done)
                    wait(d, logit_done, 2)
                    eng.copy(x2_t[:, d.slot(2), :, :].rearrange("p u t -> p (u t)"), X2T).then_inc(x2t_ready, 1)
                if z:
                    wait(z, qkv_done)
                    wait(z, ev_ready[1], RING)
                    wait(z, qk_ready[1], RING)
                    eng.copy(qkv[:, z.slot(RING), :, :], qkv_ps).then_inc(qkv_ready, 1)
                if b:
                    wait(b, on_ready)
                    wait(b, yt_done, 1)
                    for g in range(P // NH):
                        ins = eng.activation(o_g[:, :, :, g, :], o_n[:, b.slot(2), :, :, :], ACT.Copy,
                                             scale=const("group")[:, g:g + 1])
                    ins.then_inc(og_ready, 1)
                if y:
                    wait(y, y_done)
                    wait(y, x1_ready, 2)
                    eng.copy(res1[:, y.slot(2), :, :].rearrange("p u c -> p (u c)"), Y).then_inc(res1_ready, 1)
                if d:
                    wait(d, dlt_ready)
                    wait(d, w2_ready, 2)
                    eng.activation(ex[:, d.slot(2), :], dlt[:, d.slot(2), :], ACT.Exp).then_inc(ex_ready, 1)
                for n in range(3):
                    if at_step(at, MEASURE[n]):
                        eng.wait_ge(w_in[n], 16 * (1 if n < 2 else n_chunk))
                        eng.activation(absolute(n), w_new[:, :], ACT.Abs).then_inc(abs_ready, 1)

            run_steps(eng, n_duo, A_FIRST, A_LAGS, step)

            eng.wait_ge(pads_ready, 1)
            eng.wait_ge(padi_ready, 1)
            for n in range(n_exp // 2, n_exp):
                row = eng.value_load(pad_i[0:1, n:n + 1], min_val=n * region, max_val=n * region + n_tok)
                eng.dma_start(xs[bass.ds(row, TILE), :].rearrange("(u p) c -> p u c", p=P),
                              pad_rows[:, 2 * n:2 * n + 2, :]).then_inc(pads_out, 16)
            XGT = [TR, YY]
            eng.wait_ge(exp_scales, 1)

            def tile_step(at):
                if t := at(0):
                    wait(t, xgt_done)
                    wait(t, u_done[1], 2)
                    eng.mul(x_hl[:, t.slot(2), 0, :], XGT[t.slot(2)][:, 0:TILE], X_SCALE).then_inc(xhi_ready, 1)
                if t := at(2):
                    wait(t, hid_ready[1])
                    wait(t, down_done, 2)
                    eng.copy(hid_hi[:, t.slot(2), :], hid[:, t.slot(2), :]).then_inc(hhi_ready, 1)
                if t := at(1):
                    wait_ring(t, xg_in)
                    wait(t, yw_ready, RING)
                    eng.mul(xh[:, t.slot(RING), :, :], xg[:, t.slot(RING), :, 0:P], 0.5).then_inc(xh_ready, 1)
                    for half in range(2):
                        wait(t, g_done[half])
                        wait(t, hid_ready[half], 2)
                        eng.activation(sil[:, t.slot(2), 512 * half:512 * half + 512], QKV[:, 512 * half:512 * half + 512],
                                       ACT.Silu, scale=silu_scale[:, :]).then_inc(sil_ready[half], 1)

            run_steps(eng, n_tiles, B_FIRST, B_LAGS, tile_step)

            def last_norm(at):
                if c := at(2):
                    s, r = c.slot(2), c.slot(RING)
                    wait(c, fnb_ready)
                    wait_ring(c, fin_out, RING)
                    for n in range(C_SLICES):
                        ins = eng.activation(fout[:, r, n, :], fin[:, r, n, 0, :], ACT.Identity,
                                             bias=fnb[:, s, n:n + 1], scale=frs[:, s, n:n + 1])
                    ins.then_inc(fout_ready, 1)
                if c := at(3):
                    wait(c, fout_ready)
                    eng.dma_start(out_rows[:, bass.ds(c.number() * C_SLICES, C_SLICES), :],
                                  fout[:, c.slot(RING), :, :]).then_inc(fin_out[c.slot(RING)], 16)

            run_steps(eng, n_chunks_c, C_FIRST, C_LAGS, last_norm)
            for r in range(RING):
                eng.wait_ge(fin_out[r], 16 * n_chunks_c // RING)

        @block.vector
        def _(eng):
            eng.memset(ones_bf[:, :], 1.0)
            eng.wait_ge(pool_consts, 1)
            eng.wait_ge(tab_in, 16)
            eng.tensor_copy(before_bf[:, :], const("before"))
            eng.tensor_copy(cnt[:, :], const("base_e")).then_inc(consts_ready, 1)
            eng.memset(spare_rows[:, :, 0:P + 1], 0.0)
            eng.tensor_copy(spare_rows[:, :, P + 1], const("spare_ids")[:, 2 * n_exp:4 * n_exp]).then_inc(spare_ready, 1)
            eng.wait_ge(consts_ready, 1)

            def spread(it, res, stat, res_ready, stat_ready, mv_ready):
                wait(it, res_ready)
                wait(it, mv_ready, 2)
                for u in range(2):
                    ins = eng.bn_stats(stat[:, it.slot(2), u, :], res[:, it.slot(2), u, :])
                ins.then_inc(stat_ready, 1)

            def moments(it, norm, stat, stat_ready, mv_ready):
                wait(it, stat_ready)
                wait(it, nb_ready, 2 - norm)
                stand(it, norm)
                for u in range(2):
                    ins = eng.bn_aggr(mv[:, moments_slot(it, 5 + norm), norm, u, :], stat[:, it.slot(2), u, :])
                ins.then_inc(mv_ready, 1)

            def step(at):
                a, m, b, y, c, d, e = (at(lag) for lag in (2, 3, 4, 5, 6, 7, 8))

                for n in range(3):
                    if at_step(at, SPLIT[n]):
                        one = slice(n, n + 1)
                        eng.wait_ge(max_spread, n + 1)
                        eng.tensor_reduce(w_top[:, one], SPREAD, AX.X, ALU.max).then_inc(top_ready, 1)
                        eng.wait_ge(top_ready, n + 1)
                        eng.tensor_scalar(w_max[:, one], w_top[:, one], TINY, None, ALU.max).then_inc(top_kept, 1)
                        eng.wait_ge(top_kept, n + 1)
                        eng.reciprocal(w_inv[:, one], w_max[:, one]).then_inc(inv_ready, 1)
                        eng.wait_ge(inv_ready, n + 1)
                        eng.tensor_scalar(w_scale[:, one], w_inv[:, one], W_SCALE, None, ALU.mult).then_inc(scale_ready, 1)

                def times_sums(n):
                    u, h0 = n // 2, 8 * (n % 2)
                    wait(c, kv_done[n])
                    qv = xq[:, u, :].rearrange("p (h i) -> p h i", i=HD)[:, h0:h0 + 8, :]
                    eng.tensor_tensor(
                        prod_kv[:, u, 64 * h0:64 * h0 + 512].rearrange("p (h j i) -> p h j i", j=HD, i=HD),
                        KV[:, 512 * (n % 2):512 * (n % 2) + 512].rearrange("p (h j i) -> p h j i", j=HD, i=HD),
                        qv.unsqueeze(2).to_broadcast([P, 8, HD, HD]), ALU.mult).then_inc(kvp_ready[n], 1)

                if b:
                    wait(b, ev_ready[0])
                    wait(b, on_ready, 1)
                    eng.tensor_reduce(o_raw[:, 0, :], prod_ev[:, 0, :, :, :], AX.X, ALU.add).then_inc(oraw_ready[0], 1)
                if m:
                    wait(m, score_done[0])
                    wait(m, score_done[1])
                    wait(m, sub_done, 1)
                    sc = SC[:, :].rearrange("p (u i j) -> p (u i) j", u=2, j=NH)
                    eng.tensor_reduce(m_sb[:, :, :].rearrange("p u i -> p (u i)"), sc, AX.X, ALU.max).then_inc(m_ready, 1)
                if c or d:
                    slot = moments_slot(c, 5) if c else moments_slot(d, 6)
                    wait_norms(c, d, rs_ready)
                    if c:
                        wait(c, x1_ready, 2)
                    if d:
                        wait(d, x2_ready, 2)
                    eng.scalar_tensor_tensor(out=nb[:, slot, :, :], in0=mv[:, slot, :, :, 0], scalar=-1.0, in1=rs[:, slot, :, :],
                                             op0=ALU.mult, op1=ALU.mult).then_inc(nb_ready, 1)
                def divide(u):
                    wait(b, oraw_ready[u])
                    wait(b, rden_ready)
                    wait(b, og_ready, 2)
                    ins = eng.tensor_tensor(o_n[:, b.slot(2), u, :, :].rearrange("p d i -> p i d"),
                                            o_raw[:, u, :].rearrange("p (i d) -> p i d", d=HD),
                                            r_den[:, b.slot(2), u, :].unsqueeze(2).to_broadcast([P, NH, HD]), ALU.mult)
                    if u == 1:
                        ins.then_inc(on_ready, 1)

                if b:
                    wait(b, ev_ready[1])
                    eng.tensor_reduce(o_raw[:, 1, :], prod_ev[:, 1, :, :, :], AX.X, ALU.add).then_inc(oraw_ready[1], 1)
                    divide(0)
                if c:
                    s = c.slot(2)
                    wait(c, x1_ready)
                    wait(c, xq_ready, 1)
                    for u in range(2):
                        ins = eng.tensor_tensor(couples(xq_b[:, u, :]), swapped(x1[:, s, u, :]), couples(const("sq")), ALU.mult)
                    ins.then_inc(xqb_ready, 1)
                    eng.tensor_tensor(xq_a[:, :, :], x1[:, s, :, :], twice(const("cq")), ALU.mult).then_inc(xqa_ready, 1)
                if b:
                    divide(1)
                if c:
                    wait(c, xqa_ready)
                    wait(c, xqb_ready)
                    wait(c, kvp_ready[3], 1)
                    eng.tensor_tensor(xq[:, :, :], xq_a[:, :, :], xq_b[:, :, :], ALU.add).then_inc(xq_ready, 1)
                if b:
                    wait_ring(b, ctx_in)
                    wait(b, xk_ready, 1)
                    for u in range(2):
                        ins = eng.tensor_tensor(couples(xk_b[:, u, :]), swapped(ctx_sb[:, b.slot(RING), u, :]),
                                                couples(const("sk")), ALU.mult)
                    ins.then_inc(xkb_ready, 1)
                if e:
                    wait(e, ex_ready)
                    wait(e, w1_ready, 2)
                    eng.tensor_scalar(dn[:, e.slot(2), :], ex[:, e.slot(2), :], 1.0, None, ALU.add).then_inc(dn_ready, 1)
                if c:
                    wait(c, xq_ready)
                    wait(c, ret_ready, 1)
                    times_sums(0)
                if e:
                    wait(e, dn_ready)
                    eng.reciprocal(xe[:, e.slot(RING), :, 0, P], dn[:, e.slot(2), :]).then_inc(w1_ready, 1)
                if c:
                    times_sums(1)
                if e:
                    wait(e, w1_ready)
                    eng.tensor_tensor(xe[:, e.slot(RING), :, 1, P], ex[:, e.slot(2), :], xe[:, e.slot(RING), :, 0, P],
                                      ALU.mult).then_inc(w2_ready, 1)
                if a:
                    wait(a, qkv_ready)
                    for u in range(2):
                        wait(a, score_done[u], 1)
                        q = qkv[:, a.slot(RING), u, 0:P].rearrange("p (d i) -> p d i", i=NH)
                        k = qkv[:, a.slot(RING), u, P:2 * P].rearrange("p (d j) -> p d j", j=NH)
                        eng.tensor_tensor(prod_qk[:, u, :, :].rearrange("p d (i j) -> p d i j", j=NH),
                                          q.unsqueeze(3).to_broadcast([P, HD, NH, NH]),
                                          k.unsqueeze(2).to_broadcast([P, HD, NH, NH]), ALU.mult).then_inc(qk_ready[u], 1)
                if e:
                    wait(e, rank_done)
                    wait(e, cnt_ready, 1)
                    wait(e, posw_ready, 1)
                    eng.tensor_tensor(posf[:, :, :], RANK[:, 0:2 * n_exp].rearrange("p (u e) -> p u e", u=2),
                                      twice(cnt[:, :]), ALU.add).then_inc(posf_ready, 1)
                if c:
                    times_sums(2)
                if e:
                    wait(e, posf_ready)
                    eng.tensor_tensor(cnt[:, :], RANK[:, 2 * n_exp:3 * n_exp], cnt[:, :], ALU.add).then_inc(cnt_ready, 1)
                    wait(e, pos_ready, 1)
                    eng.tensor_tensor(posw[:, :, :, :], oh[:, e.slot(2), :, :, :],
                                      posf[:, :, :].unsqueeze(2).to_broadcast([P, 2, 2, n_exp]), ALU.mult).then_inc(posw_ready, 1)
                if c:
                    times_sums(3)
                if e:
                    wait(e, posw_ready)
                    wait_ring(e, routed_out, RING, 64)
                    with nc.allow_low_precision(reason="whole numbers below 2**24"):
                        eng.tensor_reduce(pos[:, e.slot(RING), :], posw[:, :, :, :].rearrange("p u k e -> p (u k) e"),
                                          AX.X, ALU.add).then_inc(pos_ready, 1)
                def sum_dims(u):
                    wait(c, kvp_ready[2 * u])
                    wait(c, kvp_ready[2 * u + 1])
                    wait(c, res2_ready, 1)
                    ins = eng.tensor_reduce(ret[:, u, :], prod_kv[:, u, :].rearrange("p (d i) -> p d i", i=HD), AX.X, ALU.add)
                    if u == 1:
                        ins.then_inc(ret_ready, 1)

                if c:
                    sum_dims(0)
                if y:
                    spread(y, res1, stat1, res1_ready, stat1_ready, mv1_ready)
                if c:
                    sum_dims(1)
                if y:
                    moments(y, 0, stat1, stat1_ready, mv1_ready)
                if d:
                    wait(d, logit_done)
                    wait(d, ix_ready, 2)
                    eng.tensor_copy(lg[:, d.slot(2), :, :].rearrange("p u e -> p (u e)"), LG).then_inc(lg_ready, 1)
                if c:
                    s = c.slot(2)
                    wait(c, ret_ready)
                    wait(c, x2_ready, 2)
                    eng.tensor_tensor(res2[:, s, :, :], ret[:, :, :], x1[:, s, :, :], ALU.add).then_inc(res2_ready, 1)
                if d:
                    wait(d, lg_ready)
                    wait(d, dlt_ready, 2)
                    stand(d, 2)
                    for u in range(2):
                        ins = eng.max(mx8[:, d.slot(2), u, :], lg[:, d.slot(2), u, :])
                    ins.then_inc(mx_ready, 1)
                if c:
                    spread(c, res2, stat2, res2_ready, stat2_ready, mv2_ready)
                if d:
                    s = d.slot(2)
                    wait(d, mx_ready)
                    wait(d, ex_ready, 2)
                    eng.tensor_tensor(dlt[:, s, :], mx8[:, s, :, 1], mx8[:, s, :, 0], ALU.subtract).then_inc(dlt_ready, 1)
                    for u in range(2):
                        ins = eng.max_index(ix8[:, s, u, :], mx8[:, s, u, :], lg[:, s, u, :])
                    ins.then_inc(ix_ready, 1)
                if c:
                    moments(c, 1, stat2, stat2_ready, mv2_ready)
                if m:
                    wait(m, e_ready)
                    wait(m, rden_ready, 1)
                    eng.tensor_reduce(den[:, :, :].rearrange("p u i -> p (u i)"),
                                      e_sb[:, m.slot(2), :, :].rearrange("p u (i j) -> p (u i) j", j=NH), AX.X,
                                      ALU.add).then_inc(den_ready, 1)
                if d:
                    s = d.slot(2)
                    wait(d, ix_ready)
                    wait(d, posw_ready, 2)
                    for u in range(2):
                        ins = eng.tensor_tensor(oh[:, s, u, :, :], twice(const("iota_e")),
                                                ix8[:, s, u, 0:2].unsqueeze(2).to_broadcast([P, 2, n_exp]), ALU.is_equal)
                    ins.then_inc(oh_ready, 1)
                if m:
                    wait(m, den_ready)
                    wait(m, on_ready, 2)
                    eng.reciprocal(r_den[:, m.slot(2), :, :], den[:, :, :]).then_inc(rden_ready, 1)
                if d:
                    wait(d, oh_ready)
                    wait(d, rank_done, 2)
                    eng.tensor_tensor(ohs[:, s, :, :], oh[:, s, :, 0, :], oh[:, s, :, 1, :], ALU.add).then_inc(ohs_ready, 1)
                for n in range(3):
                    if at_step(at, MEASURE[n]):
                        eng.wait_ge(abs_ready, n + 1)
                        eng.tensor_reduce(w_high[:, n:n + 1], absolute(n), AX.X, ALU.max).then_inc(max_ready, 1)
                        eng.wait_ge(max_ready, n + 1)
                        if n > 0:
                            eng.wait_ge(max_spread, n)
                        eng.tensor_copy(w_mats[:, :], w_high[:, n:n + 1].to_broadcast([P, P])).then_inc(mats_ready, 1)
                for n in range(3):
                    if at_step(at, SPLIT[n]):
                        eng.wait_ge(hi_ready, n + 1)
                        hl = (w1_hl, w3_hl, w2_hl)[n]
                        eng.scalar_tensor_tensor(out=hl[:, 1, :], in0=w_new[:, :], scalar=w_scale[:, n:n + 1], in1=hl[:, 0, :],
                                                 op0=ALU.mult, op1=ALU.subtract).then_inc(lo_ready, 1)
                if at_step(at, SPLIT[2]):
                    eng.wait_ge(lo_ready, 3)
                    eng.wait_ge(hi_ready, 3)
                    eng.memset(pad_rows[:, :, 0:P + 1], 0.0)
                    eng.tensor_copy(pad_rows[:, :, P + 1], const("spare_ids")[:, 0:2 * n_exp]).then_inc(pads_ready, 1)

            run_steps(eng, n_duo, A_FIRST, A_LAGS, step)

            links = [0]

            def link(ins):
                links[0] += 1
                ins.then_inc(chain, 1)
                eng.wait_ge(chain, links[0])

            link(eng.tensor_scalar(silu_scale[:, :], w_max[:, 0:1], 1.0 / (X_SCALE * W_SCALE), None, ALU.mult))
            link(eng.tensor_scalar(hid_scale[:, :], w_inv[:, 0:1], H_BOUND / (P * P * X_SCALE * W_SCALE), None, ALU.mult))
            link(eng.tensor_tensor(top13[:, :], w_max[:, 0:1], w_max[:, 1:2], ALU.mult))
            eng.scalar_tensor_tensor(out=y_scale[:, :], in0=w_max[:, 2:3], scalar=P * P / (H_BOUND * W_SCALE), in1=top13[:, :],
                                     op0=ALU.mult, op1=ALU.mult).then_inc(exp_scales, 1)
            eng.wait_ge(exp_scales, 1)

            eng.wait_ge(cnt_ready, n_duo)
            eng.tensor_copy(pad_i[:, :], cnt[:, :]).then_inc(padi_ready, 1)
            one = slice(0, 1)
            link(eng.tensor_tensor(c_cnt[one, :], cnt[one, :], const("base_e")[one, :], ALU.subtract))
            link(eng.tensor_scalar(c_int[one, :], c_cnt[one, :], float(TILE - 1), None, ALU.add))
            link(eng.tensor_scalar(c_sh[one, :], c_int[one, :], TILE.bit_length() - 1, None, ALU.logical_shift_right))
            link(eng.tensor_copy(n_t[one, :], c_sh[one, :]))
            link(eng.tensor_copy(cum[one, 0:1], n_t[one, 0:1]))
            for n in range(1, n_exp):
                link(eng.tensor_tensor(cum[one, n:n + 1], cum[one, n - 1:n], n_t[one, n:n + 1], ALU.add))
            eng.memset(t_exp[one, :], 0.0)
            link(eng.memset(t_prev[one, :], 0.0))
            no = const("tile_no")[one, :]
            for n in range(n_exp - 1):
                link(eng.tensor_scalar(t_ge[one, :], no, cum[one, n:n + 1], None, ALU.is_ge))
                link(eng.tensor_tensor(t_exp[one, :], t_exp[one, :], t_ge[one, :], ALU.add))
                link(eng.scalar_tensor_tensor(out=t_prev[one, :], in0=t_ge[one, :], scalar=n_t[one, n:n + 1],
                                              in1=t_prev[one, :], op0=ALU.mult, op1=ALU.add))
            link(eng.tensor_tensor(t_prev[one, :], no, t_prev[one, :], ALU.subtract))
            link(eng.tensor_scalar(t_base[one, :], t_exp[one, :], float(region), None, ALU.mult))
            link(eng.scalar_tensor_tensor(out=t_base[one, :], in0=t_prev[one, :], scalar=float(TILE), in1=t_base[one, :],
                                          op0=ALU.mult, op1=ALU.add))
            link(eng.tensor_scalar(t_ge[one, :], no, cum[one, n_exp - 1:n_exp], None, ALU.is_ge))
            link(eng.tensor_scalar(t_dif[one, :], no, float(TILE), float(n_exp * region - TILE * (n_tiles - n_exp)), ALU.mult, ALU.add))
            link(eng.tensor_tensor(t_dif[one, :], t_dif[one, :], t_base[one, :], ALU.subtract))
            link(eng.tensor_tensor(t_dif[one, :], t_dif[one, :], t_ge[one, :], ALU.mult))
            link(eng.tensor_tensor(t_base[one, :], t_base[one, :], t_dif[one, :], ALU.add))
            link(eng.tensor_copy(tile_base[one, :], t_base[one, :]))
            link(eng.tensor_copy(t_dif[one, 0:2], t_exp[one, 0:2]))
            link(eng.scalar_tensor_tensor(out=t_dif[one, 2:n_tiles], in0=t_exp[one, 2:n_tiles], scalar=float(n_exp),
                                          in1=t_exp[one, 0:n_tiles - 2], op0=ALU.mult, op1=ALU.add))
            link(eng.tensor_copy(two_exp[one, :], t_dif[one, :]))
            eng.tensor_copy(tile_exp[one, :], t_exp[one, :]).then_inc(table_ready, 1)

            XGT, YB = [TR, YY], [XT, SC]

            def tile_step(at):
                if t := at(0):
                    wait(t, xhi_ready)
                    eng.scalar_tensor_tensor(out=x_hl[:, t.slot(2), 1, :], in0=XGT[t.slot(2)][:, 0:TILE], scalar=X_SCALE,
                                             in1=x_hl[:, t.slot(2), 0, :], op0=ALU.mult, op1=ALU.subtract).then_inc(xlo_ready, 1)
                if t := at(2):
                    wait(t, hhi_ready)
                    eng.tensor_tensor(hid_lo[:, t.slot(2), :], hid[:, t.slot(2), :], hid_hi[:, t.slot(2), :],
                                      ALU.subtract).then_inc(hlo_ready, 1)
                if t := at(1):
                    s = t.slot(RING)
                    wait_ring(t, xg_in)
                    wait_ring(t, half_out, RING, 32)
                    eng.tensor_copy(tok_i[:, s, :], xg[:, s, :, P + 1]).then_inc(tok_ready, 1)
                    wait(t, yw_ready, RING)
                    eng.tensor_scalar(wt[:, s, :], xg[:, s, :, P], y_scale[:, :], None, ALU.mult).then_inc(wt_ready, 1)
                if t := at(3):
                    s = t.slot(RING)
                    wait(t, down_done)
                    wait(t, xh_ready)
                    wait(t, wt_ready)
                    wait_ring(t, half_out, RING, 32)
                    for u in range(2):
                        ins = eng.scalar_tensor_tensor(out=yw[:, s, u, :], in0=YB[t.slot(2)][:, P * u:P * u + P],
                                                       scalar=wt[:, s, u:u + 1], in1=xh[:, s, u, :], op0=ALU.mult, op1=ALU.add)
                    ins.then_inc(yw_ready, 1)
                if t := at(1):
                    for half in range(2):
                        cols = slice(512 * half, 512 * half + 512)
                        wait(t, u_done[half])
                        wait(t, sil_ready[half])
                        wait(t, hhi_ready, 2)
                        wait(t, hlo_ready, 2)
                        eng.scalar_tensor_tensor(out=hid[:, t.slot(2), cols], in0=KV[:, cols], scalar=hid_scale[:, :],
                                                 in1=sil[:, t.slot(2), cols], op0=ALU.mult, op1=ALU.mult).then_inc(hid_ready[half], 1)

            run_steps(eng, n_tiles, B_FIRST, B_LAGS, tile_step)

            def last_norm(at):
                if c := at(1):
                    s = c.slot(2)
                    y = fin[:, c.slot(RING), :, :, :]
                    wait_ring(c, fin_in)
                    eng.tensor_tensor(y[:, :, 0, :], y[:, :, 0, :], y[:, :, 1, :], ALU.add).then_inc(fsum_ready, 1)
                    wait(c, fsum_ready)
                    wait(c, fmv_ready, 2)
                    for n in range(C_SLICES):
                        ins = eng.bn_stats(fstat[:, s, n, :], fin[:, c.slot(RING), n, 0, :])
                    ins.then_inc(fstat_ready, 1)
                if d := at(2):
                    wait(d, frs_ready)
                    wait(d, fout_ready, 2)
                    eng.scalar_tensor_tensor(out=fnb[:, d.slot(2), :], in0=fmv[:, d.slot(2), :, 0], scalar=-1.0,
                                             in1=frs[:, d.slot(2), :], op0=ALU.mult, op1=ALU.mult).then_inc(fnb_ready, 1)
                if c:
                    wait(c, fstat_ready)
                    wait(c, fnb_ready, 2)
                    stand(c, 3)
                    for n in range(C_SLICES):
                        ins = eng.bn_aggr(fmv[:, s, n, :], fstat[:, s, n, :])
                    ins.then_inc(fmv_ready, 1)

            run_steps(eng, n_chunks_c, C_FIRST, C_LAGS, last_norm)

        @block.gpsimd
        def _(eng):
            eng.memset(eps_c[:, :], EPS)
            eng.memset(mv[:, :, :, :], 0.0)
            eng.memset(half_c[:, :], -0.5).then_inc(pool_consts, 1)
            eng.wait_ge(pool_consts, 1)
            eng.wait_ge(tab_in, 16)

            eng.wait_ge(spare_out, 16)

            def step(at):
                a, b, c, d, e = (at(lag) for lag in (3, 5, 6, 7, 8))
                if c or d:
                    slot = moments_slot(c, 5) if c else moments_slot(d, 6)
                    if c:
                        wait(c, mv1_ready)
                    if d:
                        wait(d, mv2_ready)
                    wait_norms(c, d, rs_ready, 2)
                    eng.tensor_tensor(ve[:, slot, :, :].rearrange("p k u -> p (k u)"),
                                      mv[:, slot, :, :, 1].rearrange("p k u -> p (k u)"), eps_c[:, 0:4], ALU.add).then_inc(ve_ready, 1)
                    wait_norms(c, d, ve_ready)
                    if c:
                        wait(c, x1_ready, 2)
                    if d:
                        wait(d, x2_ready, 2)
                    eng.tensor_tensor(rs[:, slot, :, :].rearrange("p k u -> p (k u)"),
                                      ve[:, slot, :, :].rearrange("p k u -> p (k u)"), half_c[:, 0:4], ALU.pow).then_inc(rs_ready, 1)
                if b:
                    wait_ring(b, ctx_in)
                    cs = ctx_sb[:, b.slot(RING), :, :]
                    wait(b, xk_ready, 1)
                    eng.tensor_tensor(xk_a[:, :, :], cs, twice(const("ck")), ALU.mult).then_inc(xka_ready, 1)
                    wait(b, xka_ready)
                    wait(b, xkb_ready)
                    wait(b, kv_ready, 1)
                    eng.tensor_tensor(xk[:, :, :], xk_a[:, :, :], xk_b[:, :, :], ALU.add).then_inc(xk_ready, 1)
                    wait(b, xk_ready)
                    wait(b, kv_done[3], 2)
                    for u in range(2):
                        ins = eng.tensor_tensor(
                            kv[:, b.slot(2), u, :].rearrange("p (h j i) -> p h j i", j=HD, i=HD),
                            xk[:, u, :].rearrange("p (h i) -> p h i", i=HD).unsqueeze(2).to_broadcast([P, NH, HD, HD]),
                            cs[:, u, :].rearrange("p (h j) -> p h j", j=HD).unsqueeze(3).to_broadcast([P, NH, HD, HD]),
                            ALU.mult)
                    ins.then_inc(kv_ready, 1)
                if a:
                    s = a.slot(2)
                    wait(a, e_ready)
                    for u in range(2):
                        wait(a, oraw_ready[u], 1)
                        eng.tensor_tensor(
                            prod_ev[:, u, :, :, :],
                            e_sb[:, s, u, :].rearrange("p (i j) -> p i j", j=NH).unsqueeze(2).to_broadcast([P, NH, HD, NH]),
                            qkv[:, a.slot(RING), u, 2 * P:3 * P].rearrange("p (d j) -> p d j", j=NH).unsqueeze(1).to_broadcast([P, NH, HD, NH]),
                            ALU.mult).then_inc(ev_ready[u], 1)
                if e:
                    r = e.slot(RING)
                    wait(e, w2_ready)
                    eng.tensor_copy(xe[:, r, :, :, P + 1],
                                    const("ids")[:, bass.ds(e.number() * 4, 4)].rearrange("p (u k) -> p u k", k=2)
                                    ).then_inc(id_ready, 1)
                    wait(e, pos_ready)
                    wait(e, id_ready)
                    stand(e, 4)
                    for n in range(4):
                        eng.indirect_dma_start(out=xs, out_offset=bass.IndirectOffsetOnAxis(ap=pos[:, r, n:n + 1], axis=0),
                                               in_=xe[:, r, n // 2, n % 2, :], in_offset=None).then_inc(routed_out[r], 16)

            run_steps(eng, n_duo, A_FIRST, A_LAGS, step)

            def scatter_tile(at):
                if t := at(3):
                    s = t.slot(RING)
                    wait(t, yw_ready)
                    wait(t, tok_ready)
                    stand(t, 5)
                    for u in range(2):
                        eng.indirect_dma_start(out=halves, out_offset=bass.IndirectOffsetOnAxis(ap=tok_i[:, s, u:u + 1], axis=0),
                                               in_=yw[:, s, u, :], in_offset=None).then_inc(half_out[s], 16)

            run_steps(eng, n_tiles, B_FIRST, B_LAGS, scatter_tile)

            def last_norm(at):
                if c := at(1):
                    s = c.slot(2)
                    wait(c, fmv_ready)
                    wait(c, frs_ready, 2)
                    eng.tensor_tensor(fve[:, s, :], fmv[:, s, :, 1], eps_c[:, 0:C_SLICES], ALU.add).then_inc(fve_ready, 1)
                    wait(c, fve_ready)
                    wait(c, fout_ready, 2)
                    eng.tensor_tensor(frs[:, s, :], fve[:, s, :], half_c[:, 0:C_SLICES], ALU.pow).then_inc(frs_ready, 1)

            run_steps(eng, n_chunks_c, C_FIRST, C_LAGS, last_norm)


def kernel(x, ctx_1024, L0_attn_Wq, L0_attn_Wk, L0_attn_Wv, L0_attn_Wo, L0_attn_bo, L0_ffn_gate,
           L0_ffn_experts_w1, L0_ffn_experts_w2, L0_ffn_experts_w3):
    import concourse.bacc as bacc
    from concourse.bass_utils import run_bass_kernel_spmd

    shape = x.shape
    n_tok = shape[0] * shape[1]
    n_exp = L0_ffn_experts_w1.shape[0]
    table, where = constants(n_tok, n_exp)
    by_dim = np.arange(P).reshape(NH, HD).T.ravel()
    w_qkv = [np.asarray(w).T[:, by_dim] for w in (L0_attn_Wq, L0_attn_Wk, L0_attn_Wv)]
    wo = np.asarray(L0_attn_Wo).T.reshape(NH, HD, P)
    arrays = {
        "x": np.asarray(x).reshape(n_tok, P),
        "ctx": np.asarray(ctx_1024).reshape(n_tok, P),
        "w_qkv": np.concatenate(w_qkv, 1),
        "wo_by_token": np.ascontiguousarray(wo[np.arange(P) % NH]),
        "bo": np.asarray(L0_attn_bo).reshape(P, 1),
        "gate": np.asarray(L0_ffn_gate),
        "w1": np.asarray(L0_ffn_experts_w1),
        "w3": np.asarray(L0_ffn_experts_w3),
        "w2": np.asarray(L0_ffn_experts_w2),
        "table": table,
    }
    nc = bacc.Bacc("TRN2", target_bir_lowering=False, num_devices=1)
    aps = {n: nc.dram_tensor(n, a.shape, mybir.dt.from_np(a.dtype), kind="ExternalInput").ap() for n, a in arrays.items()}
    out = nc.dram_tensor("out", (n_tok, P), F32, kind="ExternalOutput").ap()
    build(nc, **aps, where=where, out=out)
    result = run_bass_kernel_spmd(nc, [arrays], core_ids=[0])
    return result.results[0]["out"].reshape(shape)
```
